# Optimizing a Trainium2 kernel written in Bass

```python
import numpy as np
import jax
import jax.numpy as jnp

def _softmax(x, axis=-1):
    return jax.nn.softmax(x, axis=axis)

def _gelu(x):
    return jax.nn.gelu(x, approximate=True)

def _silu(x):
    return jax.nn.silu(x)

def _sigmoid(x):
    return jax.nn.sigmoid(x)

def _layernorm(x, axis=-1, eps=1e-05):
    m = jnp.mean(x, axis=axis, keepdims=True)
    v = jnp.var(x, axis=axis, keepdims=True)
    return (x - m) / jnp.sqrt(v + eps)

def _scatter_add(tgt, idx, src, axis=0):
    return tgt.at[idx].add(src)

def _segment_sum(src, seg, n):
    return jax.ops.segment_sum(src, seg, n)
kernel_name = 'mk_pixart_seq_d1_seqx_r4_5fe24f'

def setup_inputs(seed: int=0):
    np.random.seed(seed)
    _w = jnp.asarray

    def _rec_inputs():
        import jax
        import jax.numpy as jnp
        _rk = jax.random.key(seed)
        x = -0.0002928 + 1 * jax.random.normal(jax.random.fold_in(_rk, 1), (16, 256, 256), jnp.float32)
        _lenS = 256 - jax.random.randint(jax.random.fold_in(_rk, 7), (16,), 0, max(1, 256 // 4) + 1, jnp.int32)
        _lenS2 = 256 - jax.random.randint(jax.random.fold_in(_rk, 8), (16,), 0, max(1, 256 // 4) + 1, jnp.int32)
        cond_1024 = 0.0061147 + 1.02565 * jax.random.normal(jax.random.fold_in(_rk, 11), (16, 256), jnp.float32)
        _ctx_1024P = jax.random.normal(jax.random.fold_in(_rk, 12), (16, 16, 256), jnp.float32)
        _ctx_1024c = jax.random.dirichlet(jax.random.fold_in(_rk, 512), 0.3 * jnp.ones((16,), jnp.float32), (16, 256))
        _ctx_1024t = jnp.einsum('bsk,bkd->bsd', _ctx_1024c, _ctx_1024P)
        _ctx_1024t = _ctx_1024t * jax.lax.rsqrt(jnp.mean(jnp.square(_ctx_1024t)) + 1e-12) * 0.953939
        ctx_1024 = -0.00265004 + 0.998804 * (_ctx_1024t + 0.3 * jax.random.normal(jax.random.fold_in(_rk, 612), (16, 256, 256), jnp.float32))
        return (x, cond_1024, ctx_1024)
    x, cond_1024, ctx_1024 = _rec_inputs()

    def _L0_xcond_setup():
        import jax, jax.numpy as jnp
        import numpy as np
        LN_EPS = 1e-06

        def _ln(x):
            mu = jnp.mean(x, axis=-1, keepdims=True)
            var = jnp.var(x, axis=-1, keepdims=True)
            return (x - mu) * jax.lax.rsqrt(var + LN_EPS)
        key = jax.random.key(seed)
        H, NH = (256, 16)
        B, N, S = (4, 256, 77)
        MLP = int(H * 4.0)
        ks = jax.random.split(key, 20)
        s = 1.0 / np.sqrt(H)
        return {'x': jax.random.normal(ks[0], (B, N, H), jnp.float32), 'c': jax.random.normal(ks[1], (B, H), jnp.float32), 'context': jax.random.normal(ks[2], (B, S, H), jnp.float32), 'W_mod': jax.random.normal(ks[3], (H, 6 * H), jnp.float32) * s, 'b_mod': jnp.zeros((6 * H,), jnp.float32), 'W_qkv': jax.random.normal(ks[4], (H, 3 * H), jnp.float32) * s, 'b_qkv': jnp.zeros((3 * H,), jnp.float32), 'W_proj': jax.random.normal(ks[5], (H, H), jnp.float32) * s, 'b_proj': jnp.zeros((H,), jnp.float32), 'W_qc': jax.random.normal(ks[6], (H, H), jnp.float32) * s, 'b_qc': jnp.zeros((H,), jnp.float32), 'W_kvc': jax.random.normal(ks[7], (H, 2 * H), jnp.float32) * s, 'b_kvc': jnp.zeros((2 * H,), jnp.float32), 'W_cproj': jax.random.normal(ks[8], (H, H), jnp.float32) * s, 'b_cproj': jnp.zeros((H,), jnp.float32), 'W_mlp1': jax.random.normal(ks[9], (H, MLP), jnp.float32) * s, 'b_mlp1': jnp.zeros((MLP,), jnp.float32), 'W_mlp2': jax.random.normal(ks[10], (MLP, H), jnp.float32) * (1.0 / np.sqrt(MLP)), 'b_mlp2': jnp.zeros((H,), jnp.float32)}
    _L0_xcond_all = _L0_xcond_setup()
    _L0_xcond_in = {k: v for k, v in _L0_xcond_all.items() if k in ('W_mod', 'b_mod', 'W_qkv', 'b_qkv', 'W_proj', 'b_proj', 'W_qc', 'b_qc', 'W_kvc', 'b_kvc', 'W_cproj', 'b_cproj', 'W_mlp1', 'b_mlp1', 'W_mlp2', 'b_mlp2')}
    del _L0_xcond_all
    return {'x': x, 'cond_1024': cond_1024, 'ctx_1024': ctx_1024, 'L0_xcond_W_mod': _L0_xcond_in['W_mod'], 'L0_xcond_b_mod': _L0_xcond_in['b_mod'], 'L0_xcond_W_qkv': _L0_xcond_in['W_qkv'], 'L0_xcond_b_qkv': _L0_xcond_in['b_qkv'], 'L0_xcond_W_proj': _L0_xcond_in['W_proj'], 'L0_xcond_b_proj': _L0_xcond_in['b_proj'], 'L0_xcond_W_qc': _L0_xcond_in['W_qc'], 'L0_xcond_b_qc': _L0_xcond_in['b_qc'], 'L0_xcond_W_kvc': _L0_xcond_in['W_kvc'], 'L0_xcond_b_kvc': _L0_xcond_in['b_kvc'], 'L0_xcond_W_cproj': _L0_xcond_in['W_cproj'], 'L0_xcond_b_cproj': _L0_xcond_in['b_cproj'], 'L0_xcond_W_mlp1': _L0_xcond_in['W_mlp1'], 'L0_xcond_b_mlp1': _L0_xcond_in['b_mlp1'], 'L0_xcond_W_mlp2': _L0_xcond_in['W_mlp2'], 'L0_xcond_b_mlp2': _L0_xcond_in['b_mlp2']}

def reference(x, cond_1024, ctx_1024, L0_xcond_W_mod, L0_xcond_b_mod, L0_xcond_W_qkv, L0_xcond_b_qkv, L0_xcond_W_proj, L0_xcond_b_proj, L0_xcond_W_qc, L0_xcond_b_qc, L0_xcond_W_kvc, L0_xcond_b_kvc, L0_xcond_W_cproj, L0_xcond_b_cproj, L0_xcond_W_mlp1, L0_xcond_b_mlp1, L0_xcond_W_mlp2, L0_xcond_b_mlp2):
    import jax
    import jax.numpy as jnp

    def _L0_xcond_ref(x, c, context, W_mod, b_mod, W_qkv, b_qkv, W_proj, b_proj, W_qc, b_qc, W_kvc, b_kvc, W_cproj, b_cproj, W_mlp1, b_mlp1, W_mlp2, b_mlp2):
        import jax, jax.numpy as jnp
        import numpy as np
        LN_EPS = 1e-06

        def _ln(x):
            mu = jnp.mean(x, axis=-1, keepdims=True)
            var = jnp.var(x, axis=-1, keepdims=True)
            return (x - mu) * jax.lax.rsqrt(var + LN_EPS)
        B, N, H = x.shape
        NH = 16
        hd = H // NH
        scale = hd ** (-0.5)
        c_proj = jax.nn.silu(c) @ W_mod + b_mod
        shift_a, scale_a, gate_a, shift_m, scale_m, gate_m = jnp.split(c_proj, 6, axis=-1)

        def modulate(t, shift, sc):
            return t * (1 + sc[:, None]) + shift[:, None]
        x_norm = modulate(_ln(x), shift_a, scale_a)
        qkv = x_norm @ W_qkv + b_qkv
        q, k, v = jnp.split(qkv, 3, axis=-1)
        q = q.reshape(B, N, NH, hd).transpose(0, 2, 1, 3)
        k = k.reshape(B, N, NH, hd).transpose(0, 2, 1, 3)
        v = v.reshape(B, N, NH, hd).transpose(0, 2, 1, 3)
        attn_w = jax.nn.softmax(jnp.einsum('bhqd,bhkd->bhqk', q, k) * scale, axis=-1)
        attn_out = jnp.einsum('bhqk,bhkd->bhqd', attn_w, v)
        attn_out = attn_out.transpose(0, 2, 1, 3).reshape(B, N, H)
        attn_out = attn_out @ W_proj + b_proj
        x = x + gate_a[:, None] * attn_out
        S = context.shape[1]
        q_c = _ln(x) @ W_qc + b_qc
        kv_c = _ln(context) @ W_kvc + b_kvc
        k_c, v_c = jnp.split(kv_c, 2, axis=-1)
        q_c = q_c.reshape(B, N, NH, hd).transpose(0, 2, 1, 3)
        k_c = k_c.reshape(B, S, NH, hd).transpose(0, 2, 1, 3)
        v_c = v_c.reshape(B, S, NH, hd).transpose(0, 2, 1, 3)
        c_attn_w = jax.nn.softmax(jnp.einsum('bhqd,bhsd->bhqs', q_c, k_c) * scale, axis=-1)
        c_attn_out = jnp.einsum('bhqs,bhsd->bhqd', c_attn_w, v_c)
        c_attn_out = c_attn_out.transpose(0, 2, 1, 3).reshape(B, N, H)
        c_attn_out = c_attn_out @ W_cproj + b_cproj
        x = x + c_attn_out
        x_norm2 = modulate(_ln(x), shift_m, scale_m)
        h = jax.nn.gelu(x_norm2 @ W_mlp1 + b_mlp1)
        h = h @ W_mlp2 + b_mlp2
        x = x + gate_m[:, None] * h
        return x
    x = _L0_xcond_ref(x, cond_1024, ctx_1024, L0_xcond_W_mod, L0_xcond_b_mod, L0_xcond_W_qkv, L0_xcond_b_qkv, L0_xcond_W_proj, L0_xcond_b_proj, L0_xcond_W_qc, L0_xcond_b_qc, L0_xcond_W_kvc, L0_xcond_b_kvc, L0_xcond_W_cproj, L0_xcond_b_cproj, L0_xcond_W_mlp1, L0_xcond_b_mlp1, L0_xcond_W_mlp2, L0_xcond_b_mlp2)
    return x

_drawn_inputs = setup_inputs


def setup_inputs(seed=0):
    import zlib

    import numpy as np

    out = dict(_drawn_inputs(seed))
    spreads = {'L0_xcond_b_mod': (0.0, 0.1),
     'L0_xcond_b_qkv': (0.0, 0.1),
     'L0_xcond_b_proj': (0.0, 0.1),
     'L0_xcond_b_qc': (0.0, 0.571),
     'L0_xcond_b_kvc': (0.0, 0.1),
     'L0_xcond_b_cproj': (0.0, 0.1),
     'L0_xcond_b_mlp1': (0.0, 0.1),
     'L0_xcond_b_mlp2': (0.0, 0.1)}
    factors = {}
    for name, (base, spread) in spreads.items():
        noise = np.random.default_rng([zlib.crc32(name.encode()), seed]).standard_normal(out[name].shape)
        drawn = base * np.exp(spread * noise) if base else spread * noise
        out[name] = jnp.asarray(drawn.astype(out[name].dtype))
    for name, factor in factors.items():
        out[name] = (out[name] * factor).astype(out[name].dtype)
    return out
```

```python
import concourse.bass as bass
from concourse import mybir
from contextlib import ExitStack

fp32 = mybir.dt.float32
f32r = mybir.dt.float32r
ALU = mybir.AluOpType
ACT = mybir.ActivationFunctionType
AXIS = mybir.AxisListType

B, N, H, NH, MLP = 16, 256, 256, 16, 1024
HD = H // NH
CB = H // 128
NB = N // 128
FB = MLP // 128
PAIRS = NH // 2
EPS = 1e-6
SCALE = HD ** -0.5
HI, LO = 0, 1

STAGES = [
    ("norm_y", -1),
    ("scan_x", 0),
    ("attend_y", -2),
    ("project_y", -1),
    ("max_x", 0),
    ("out_y", -2),
    ("norm_x", 1),
    ("mlp_up", -2),
    ("scan_y", -1),
    ("attend_x", 0),
    ("project_x", 1),
    ("max_y", -1),
    ("out_x", 0),
    ("mlp_down", -2),
]
RANK = {name: i for i, (name, _) in enumerate(STAGES)}
SHIFT = dict(STAGES)
FIRST, LAST = -1, B + 1
LOOP = (3, B - 1)

BANK_USES = {"norm_y": 2, "project_y": 3, "max_x": 1, "out_y": 2, "norm_x": 1, "mlp_up": 4,
             "project_x": 3, "max_y": 1, "out_x": 1, "mlp_down": 2}
ACT_USES = {"norm_y": 2, "project_y": 2, "out_y": 1, "norm_x": 1, "mlp_up": 4, "project_x": 2}
SCANS = {"scan_x": NH, "scan_y": NH}
ATTENDS = {"attend_x": NH, "attend_y": NH}
GROUPS = {"attend_x": 4, "attend_y": 4}
HALVES = {"attend_x": 2, "attend_y": 2}
NORMS = {"norm_y": 1, "out_y": 1, "norm_x": 1}
STORES = {"project_x": 2, "project_y": 2}
LOADS_X, LOADS_Y = {"project_x": 12}, {"project_y": 12}
ROWS = {"max_x": 4, "max_y": 4}
LINKS = {"norm_y": 1, "out_y": 2, "norm_x": 2, "attend_x": 8, "attend_y": 8, "max_x": 1, "max_y": 1}


def build(nc, x, cond, ctx_in, W_mod, b_mod, W_qkv, b_qkv, W_proj, b_proj, W_qc, b_qc, W_kvc, b_kvc,
          W_cproj, b_cproj, W_mlp1, b_mlp1, W_mlp2, b_mlp2, out):
    def before(per, t, stage):
        def at(step, clamp):
            total = 0
            for name, n in per.items():
                ran = step + SHIFT[name] + (1 if RANK[name] < RANK[stage] else 0)
                total += n * (min(max(ran, 0), B) if clamp else ran)
            return total
        if isinstance(t, int):
            return at(t, True)
        slope = at(3, False) - at(2, False)
        base = at(2, False) - 2 * slope
        return t * slope + base if slope else base

    def bank_of(t, stage, use):
        return (before(BANK_USES, t if isinstance(t, int) else LOOP[0], stage) + use) % 2

    def wait(eng, sem, value):
        if not isinstance(value, int) or value > 0:
            eng.wait_ge(sem, value)

    def head_of(half, g, j):
        return (2 * (2 * half + g) + j // 2) + PAIRS * (j % 2)

    es = ExitStack()
    with es:
        def sb(name, shape, dt=fp32):
            return es.enter_context(nc.sbuf_tensor(name, shape, dt))

        def sem(name):
            return es.enter_context(nc.semaphore(name))

        def dram(name, shape, dt=fp32):
            return nc.dram_tensor(name, shape, dt, kind="Internal").ap()

        WT = sb("WT", [128, 2, 4 * 2048], f32r)

        def weight(start, blocks, cols):
            return [WT[:, part, start:start + blocks * cols].rearrange("p (c n) -> p c n", c=blocks)
                    for part in (HI, LO)]

        w_qkv = weight(0, CB, 3 * H)
        w_qc = weight(1536, CB, H)
        w_kvc = weight(2048, CB, 2 * H)
        w_proj = weight(3072, 2, H)
        w_cproj = weight(3584, 2, H)
        w_mlp1 = weight(4096, CB, MLP)
        w_mlp2 = weight(6144, FB, H)

        QS = {s: sb(f"QS_{s}", [128, PAIRS, N], f32r) for s in "xy"}
        KS = {s: sb(f"KS_{s}", [128, PAIRS, N], f32r) for s in "xy"}
        V = {s: sb(f"V_{s}", [128, NB, NH, 32]) for s in "xy"}
        P = sb("P", [128, 8, NB, N])
        SQ = sb("SQ", [128, 2, 2, N], f32r)
        SK = sb("SK", [128, 2, 2, N], f32r)
        xT_x = sb("xT_x", [128, 2, CB, N], f32r)
        xT_y = sb("xT_y", [128, 2, CB, N], f32r)
        xT_c = sb("xT_c", [128, 2, CB, N], f32r)
        HH = sb("HH", [128, 2, FB, N], f32r)
        HF = sb("HF", [128, 2, 2, N])
        xn_a = sb("xn_a", [128, NB, H])
        xn_b = sb("xn_b", [128, NB, H])
        x_in = sb("x_in", [128, NB, H])
        c_in = sb("c_in", [128, NB, H])
        x1 = sb("x1", [128, NB, H])
        x1_bias = sb("x1_bias", [128, NB, H])
        x2 = sb("x2", [128, NB, H])
        x2_bias = sb("x2_bias", [128, NB, H])
        x_bias = sb("x_bias", [128, NB, H])
        y = sb("y", [128, NB, H])
        gated = sb("gated", [128, NB, H])
        xm = sb("xm", [128, CB, N])
        PT = sb("PT", [128, 2, 8, 32])
        PN = sb("PN", [128, 8, 2, HD])
        PO = sb("PO", [128, N])
        OT = sb("OT", [128, 2, 2, N], f32r)
        rsum = sb("rsum", [128, 2, 8])
        MX = sb("MX", [128, NB, 2, PAIRS])
        MH = sb("MH", [128, NB, 2, NH], f32r)
        MT = sb("MT", [2 * NH, N], f32r)
        stats = sb("stats", [128, 4, 6])
        mv = sb("mv", [128, 4, 2])
        rstd = sb("rstd", [128, 4])
        var_eps = sb("var_eps", [128, 4])
        minus_half = sb("minus_half", [128, 4])
        eps = sb("eps", [128, 4])
        spare = sb("spare", [128, 1])
        ident = sb("ident", [128, 128])
        bias_rows = sb("bias_rows", [32, 128])
        bias_cols = sb("bias_cols", [128, 32])
        bc_v = {"x": sb("bc_v_x", [128, H]), "y": sb("bc_v_y", [128, H])}
        bc_proj = sb("bc_proj", [128, H])
        bc_cproj = sb("bc_cproj", [128, H])
        bc_mlp2 = sb("bc_mlp2", [128, H])
        gb_a = sb("gb_a", [128, H])
        gb_m = sb("gb_m", [128, H])
        gate_a = sb("gate_a", [128, H])
        gate_m = sb("gate_m", [128, H])
        mod_x = sb("mod_x", [128, 4])
        mod_m = sb("mod_m", [128, 4])
        cond_sb = HF[0:B, :, :, :].rearrange("p a b c -> p (a b) c")
        silu_T = sb("silu_T", [128, CB, B])
        mod_all = sb("mod_all", [128, B, 8])
        gate_bias = x2_bias[0:B, :, :].rearrange("p a c -> p (a c)")
        gate_all = x2[0:B, :, :].rearrange("p a c -> p (a c)")

        d_mod = dram("d_mod", (B, 128, 8))
        d_gate = dram("d_gate", (B, 2 * H))
        d_q = {s: dram(f"d_q_{s}", (2, 2, 128, N)) for s in "xy"}
        d_k = {s: dram(f"d_k_{s}", (2, 2, 128, N)) for s in "xy"}

        scan_bank = [es.enter_context(nc.psum_tensor(f"scan{i}", [128, 512], fp32)) for i in range(2)]
        score_bank = [es.enter_context(nc.psum_tensor(f"score{i}", [128, 512], fp32)) for i in range(2)]
        pv_bank = [es.enter_context(nc.psum_tensor(f"pv{i}", [128, 512], fp32)) for i in range(2)]
        bank = [es.enter_context(nc.psum_tensor(f"bank{i}", [128, 512], fp32)) for i in range(2)]

        s_ident = sem("s_ident")
        s_const = sem("s_const")
        s_small = sem("s_small")
        s_wmod = sem("s_wmod")
        s_weight = [sem(f"s_weight{i}") for i in range(4)]
        s_weight_hi = sem("s_weight_hi")
        s_weight_lo = sem("s_weight_lo")
        s_silu = sem("s_silu")
        s_silu_part = sem("s_silu_part")
        s_exp0 = sem("s_exp0")
        s_startT = sem("s_startT")
        s_startC = sem("s_startC")
        s_mod = sem("s_mod")
        s_modC = sem("s_modC")
        s_modD = sem("s_modD")
        s_x = sem("s_x")
        s_modx = sem("s_modx")
        s_c = sem("s_c")
        s_gate_a = sem("s_gate_a")
        s_gate_m = sem("s_gate_m")
        s_modm = sem("s_modm")
        s_bank_full = sem("s_bank_full")
        s_bank_hi = sem("s_bank_hi")
        s_bank_done = sem("s_bank_done")
        s_scan_full = sem("s_scan_full")
        s_scan_done = sem("s_scan_done")
        s_score_full = sem("s_score_full")
        s_exp = sem("s_exp")
        s_pv = sem("s_pv")
        s_pv_read = sem("s_pv_read")
        s_OT = sem("s_OT")
        s_max = sem("s_max")
        s_row = sem("s_row")
        s_store = sem("s_store")
        s_load = {"x": sem("s_load_x"), "y": sem("s_load_y")}
        s_mv = sem("s_mv")
        s_eps = sem("s_eps")
        s_rstd = sem("s_rstd")
        s_xn_y, s_xn_c, s_xn_m, s_xn_x = sem("s_xn_y"), sem("s_xn_c"), sem("s_xn_m"), sem("s_xn_x")
        s_x_bias = sem("s_x_bias")
        s_x1 = sem("s_x1")
        s_x1_bias = sem("s_x1_bias")
        s_x2_bias = sem("s_x2_bias")
        s_hidden_lo = sem("s_hidden_lo")
        s_y = sem("s_y")
        s_out = sem("s_out")
        s_link = sem("s_link")
        s_pool = sem("s_pool")

        block = es.enter_context(nc.Block())

        def steps(eng, step):
            for t in range(FIRST, LOOP[0]):
                yield_step(step, t)
            with eng.Fori(LOOP[0], LOOP[1]) as t:
                step(t, lambda name: True)
            for t in range(LOOP[1], LAST + 1):
                yield_step(step, t)

        def yield_step(step, t):
            step(t, lambda name: 0 <= t + SHIFT[name] < B)

        MODC, QKVC, QCC, KVCC, MLPC = 0, 12, 18, 20, 24
        PARTS = ((HI, HI), (HI, LO), (LO, HI))

        @block.sync
        def _(sp):
            sp.dma_start(cond_sb[:, 0, :], cond).then_inc(s_small, 16)
            for start, src in ((MODC, b_mod), (QKVC, b_qkv), (QCC, b_qc), (KVCC, b_kvc), (MLPC, b_mlp1)):
                rows = src.rearrange("(k p) -> k p", p=128)
                sp.dma_start(bias_rows[start:start + rows.shape[0], :], rows).then_inc(s_small, 16)
            for i in range(2):
                sp.dma_start(gate_bias[:, i * H:(i + 1) * H],
                             b_mod[(3 * i + 2) * H:(3 * i + 3) * H].partition_broadcast(B)).then_inc(s_small, 16)
            stage_w = P[:, :, :, :].rearrange("p a b c -> p (a b c)")
            sp.dma_start(stage_w[:, 0:CB * 6 * H].rearrange("p (c n) -> p c n", c=CB),
                         W_mod.rearrange("(c p) n -> p c n", p=128)).then_inc(s_wmod, 16)
            for dst, src in ((bc_v["x"], b_qkv[2 * H:3 * H]), (bc_v["y"], b_kvc[H:2 * H]), (bc_proj, b_proj),
                             (bc_cproj, b_cproj), (bc_mlp2, b_mlp2)):
                sp.dma_start(dst[:, :], src.partition_broadcast(128)).then_inc(s_const, 16)

            def load_weights(i):
                if i < 2:
                    sp.wait_ge(s_mod, 2)
                else:
                    sp.wait_ge(s_weight_lo, i - 1)
                to = stage_w[:, (i % 2) * 2048:(i % 2 + 1) * 2048]
                if i == 0:
                    sp.dma_start(to[:, 0:1536].rearrange("p (c n) -> p c n", c=CB),
                                 W_qkv.rearrange("(c p) n -> p c n", p=128)).then_inc(s_weight[i], 16)
                    sp.dma_start(to[:, 1536:2048].rearrange("p (c n) -> p c n", c=CB),
                                 W_qc.rearrange("(c p) n -> p c n", p=128)).then_inc(s_weight[i], 16)
                elif i == 1:
                    sp.dma_start(to[:, 0:1024].rearrange("p (c n) -> p c n", c=CB),
                                 W_kvc.rearrange("(c p) n -> p c n", p=128)).then_inc(s_weight[i], 16)
                    for k, w in enumerate((W_proj, W_cproj)):
                        dst = to[:, 1024 + 512 * k:1536 + 512 * k].rearrange("p (c n) -> p c n", c=2)
                        for g in range(2):
                            for j in range(4):
                                row = 32 * j + HD * g
                                for half in range(2):
                                    head = head_of(half, g, j)
                                    sp.dma_start(dst[row:row + HD, half, :],
                                                 w[head * HD:(head + 1) * HD, :]).then_inc(s_weight[i], 16)
                elif i == 2:
                    sp.dma_start(to.rearrange("p (c n) -> p c n", c=CB),
                                 W_mlp1.rearrange("(c p) n -> p c n", p=128)).then_inc(s_weight[i], 16)
                else:
                    sp.dma_start(to.rearrange("p (c n) -> p c n", c=FB),
                                 W_mlp2.rearrange("(c p) n -> p c n", p=128)).then_inc(s_weight[i], 16)

            sp.wait_ge(s_modC, 1)
            sp.dma_start(d_mod.rearrange("b p k -> p b k"), mod_all[:, :, :]).then_inc(s_modD, 16)
            sp.wait_ge(s_modC, 2)
            sp.dma_start(d_gate, gate_all).then_inc(s_modD, 16)
            load_weights(0)
            sp.wait_ge(s_modD, 32)

            def stacks(t, stage, s, attend):
                first = before(BANK_USES, t, stage)
                stored = before(STORES, t, stage)
                for i, (d, src) in enumerate(((d_q[s], SQ), (d_k[s], SK))):
                    sp.wait_ge(s_bank_done, first + i + 1)
                    sp.dma_start(d.rearrange("a c p n -> p (a c) n"),
                                 src[:, :, :, :].rearrange("p a c n -> p (a c) n").bitcast(fp32)).then_inc(s_store, 16)
                wait(sp, s_score_full, before(ATTENDS, t, stage))
                for i, (d, dst, parts) in enumerate(((d_q[s], QS[s], (HI, HI, LO)), (d_k[s], KS[s], (HI, LO, HI)))):
                    if i == 0:
                        sp.wait_ge(s_store, stored * 16 + 32)
                    for par in range(2):
                        for c, part in enumerate(parts):
                            row = 64 * par + HD * c
                            sp.dma_start(dst[row:row + HD, :, :].bitcast(fp32),
                                         d[part, par].rearrange("(p d) n -> d p n", d=HD)).then_inc(s_load[s], 16)

            def rows(t, stage, s):
                sp.wait_ge(s_bank_done, before(BANK_USES, t, stage) + 1)
                for par in range(2):
                    for part in (HI, LO):
                        row = 64 * par + 3 * HD + part
                        src = part * NH + par * PAIRS
                        sp.dma_start(QS[s][row:row + 1, :, :].bitcast(fp32),
                                     MT[src:src + PAIRS, :].bitcast(fp32)).then_inc(s_row, 16)

            def step(t, has):
                if has("out_x"):
                    wait(sp, s_x1, t)
                    sp.dma_start(gate_a[:, :], d_gate[t, 0:H].partition_broadcast(128)).then_inc(s_gate_a, 16)
                if has("out_y"):
                    wait(sp, s_y, (t - 2) * 2)
                    sp.dma_start(gate_m[:, :], d_gate[t - 2, H:2 * H].partition_broadcast(128)).then_inc(s_gate_m, 16)
                    sp.dma_start(mod_m[:, :], d_mod[t - 2, :, 4:8]).then_inc(s_modm, 16)
                if has("norm_x"):
                    wait(sp, s_x_bias, t + 1)
                    sp.dma_start(x_in[:, :, :], x[t + 1].rearrange("(a p) c -> p a c", p=128)).then_inc(s_x, 16)
                    sp.dma_start(mod_x[:, :], d_mod[t + 1, :, 0:4]).then_inc(s_modx, 16)
                if has("out_x"):
                    wait(sp, s_xn_c, t)
                    sp.dma_start(c_in[:, :, :], ctx_in[t].rearrange("(a p) c -> p a c", p=128)).then_inc(s_c, 16)
                if has("project_y"):
                    stacks(t, "project_y", "y", "attend_y")
                if has("max_x"):
                    rows(t, "max_x", "x")
                if has("project_x"):
                    stacks(t, "project_x", "x", "attend_x")
                if has("max_y"):
                    rows(t, "max_y", "y")
                if has("mlp_down"):
                    sp.wait_ge(s_y, (t - 2) * 2 + 2)
                    sp.dma_start(out[t - 2].rearrange("(a p) c -> p a c", p=128), y[:, :, :]).then_inc(s_out, 16)
                if isinstance(t, int) and t == FIRST:
                    for i in range(1, 4):
                        load_weights(i)

            steps(sp, step)
            sp.wait_ge(s_out, 16 * B)

        @block.gpsimd
        def _(pool):
            nc.gpsimd.memset(ident[:, :], 0.0).then_inc(s_pool, 1)
            pool.wait_ge(s_pool, 1)
            nc.gpsimd.affine_select(out=ident[:, :], in_=ident[:, :], compare_op=ALU.not_equal, fill=1.0, base=0,
                                    pattern=[[-1, 128]], channel_multiplier=1).then_inc(s_ident, 1)
            nc.gpsimd.memset(V["x"][:, :, :, :], 1.0)
            nc.gpsimd.memset(V["y"][:, :, :, :], 1.0).then_inc(s_ident, 1)
            nc.gpsimd.memset(KS["x"][:, :, :].bitcast(fp32), 1.0)
            nc.gpsimd.memset(KS["y"][:, :, :].bitcast(fp32), 1.0).then_inc(s_ident, 1)
            nc.gpsimd.memset(eps[:, :], EPS)
            nc.gpsimd.memset(minus_half[:, :], -0.5).then_inc(s_ident, 1)
            pool.wait_ge(s_ident, 4)
            pool.wait_ge(s_const, 16 * 5)

            def deviation(t, stage, n):
                pool.wait_ge(s_mv, before(NORMS, t, stage) + 1)
                nc.gpsimd.tensor_tensor(var_eps[:, 0:n], mv[:, 0:n, 1], eps[:, 0:n], ALU.add).then_inc(s_eps, 1)
                pool.wait_ge(s_eps, before(NORMS, t, stage) + 1)
                nc.gpsimd.tensor_tensor(rstd[:, 0:n], var_eps[:, 0:n], minus_half[:, 0:n], ALU.pow).then_inc(s_rstd, 1)

            def step(t, has):
                if has("norm_y"):
                    deviation(t, "norm_y", 4)
                if has("out_x"):
                    pool.wait_ge(s_gate_a, t * 16 + 16)
                    pool.wait_ge(s_x, t * 16 + 16)
                    nc.gpsimd.tensor_tensor(gb_a[:, :], gate_a[:, :], bc_proj[:, :], ALU.mult).then_inc(s_pool, 1)
                    wait(pool, s_x1, t)
                    pool.wait_ge(s_pool, links(t, "x") + 2)
                    for a in range(NB):
                        last = nc.gpsimd.tensor_tensor(x_bias[:, a, :], x_in[:, a, :], gb_a[:, :], ALU.add)
                    last.then_inc(s_x_bias, 1)
                if has("out_y"):
                    deviation(t, "out_y", 2)
                if has("norm_y"):
                    if has("out_y"):
                        pool.wait_ge(s_bank_done, before(BANK_USES, t, "out_y") + 1)
                    pool.wait_ge(s_x1, t)
                    for a in range(NB):
                        last = nc.gpsimd.tensor_tensor(x1_bias[:, a, :], x1[:, a, :], bc_cproj[:, :], ALU.add)
                    last.then_inc(s_x1_bias, 1)
                if has("norm_x"):
                    deviation(t, "norm_x", 2)
                if has("out_y"):
                    pool.wait_ge(s_gate_m, (t - 2) * 16 + 16)
                    nc.gpsimd.tensor_tensor(gb_m[:, :], gate_m[:, :], bc_mlp2[:, :], ALU.mult).then_inc(s_pool, 1)
                    pool.wait_ge(s_bank_done, before(BANK_USES, t, "out_y") + 1)
                    pool.wait_ge(s_pool, links(t, "m") + 2)
                    for a in range(NB):
                        last = nc.gpsimd.tensor_tensor(x2_bias[:, a, :], x2[:, a, :], gb_m[:, :], ALU.add)
                    last.then_inc(s_x2_bias, 1)
                if has("mlp_up"):
                    for u in range(FB // 2):
                        pool.wait_ge(s_bank_done, before(BANK_USES, t, "mlp_up") + u + 1)
                        nc.gpsimd.tensor_tensor(HH[:, LO, 2 * u:2 * u + 2, :], HF[:, u % 2, :, :],
                                                HH[:, HI, 2 * u:2 * u + 2, :].bitcast(fp32),
                                                ALU.subtract).then_inc(s_hidden_lo, 1)

            def links(t, which):
                if which == "x":
                    return before({"out_x": 1, "out_y": 1}, t, "norm_y")
                return before({"out_x": 1, "out_y": 1}, t, "norm_y") + (1 if not isinstance(t, int) or t < B else 0)

            steps(pool, step)

        @block.tensor
        def _(pe):
            pe.wait_ge(s_ident, 3)
            pe.wait_ge(s_small, 16 * 8)
            nc.tensor.transpose(scan_bank[0][:, 0:32], bias_rows[:, :], ident[0:32, 0:32])
            pe.wait_ge(s_silu, 1)
            for c in range(CB):
                last = nc.tensor.transpose(scan_bank[1][:, c * B:(c + 1) * B],
                                           cond_sb[:, 2, c * 128:(c + 1) * 128], ident[0:B, 0:B])
            last.then_inc(s_startT, 1)
            pe.wait_ge(s_startC, 1)
            pe.wait_ge(s_wmod, 16)
            wmod = P[:, :, :, :].rearrange("p a b c -> p (a b c)")[:, 0:CB * 6 * H].rearrange("p (c n) -> p c n", c=CB)
            for k, blk in enumerate((0, 1, 2, 3, 6, 7, 8, 9)):
                for c in range(CB):
                    last = nc.tensor.matmul(score_bank[0][:, k * B:(k + 1) * B], wmod[:, c, blk * 128:(blk + 1) * 128],
                                            silu_T[:, c, :], start=(c == 0), stop=(c == CB - 1))
            last.then_inc(s_mod, 1)
            for i in range(2):
                for c in range(CB):
                    last = nc.tensor.matmul(score_bank[1][0:B, i * H:(i + 1) * H], silu_T[:, c, :],
                                            wmod[:, c, (3 * i + 2) * H:(3 * i + 3) * H],
                                            start=(c == 0), stop=(c == CB - 1))
            last.then_inc(s_mod, 1)
            pe.wait_ge(s_modC, 2)

            def take(t, stage, use):
                wait(pe, s_bank_done, before(BANK_USES, t, stage) + use - 1)
                return bank[bank_of(t, stage, use)]

            def transposes(t, stage, use, src):
                to = take(t, stage, use)
                for c in range(CB):
                    for a in range(NB):
                        last = nc.tensor.transpose(to[:, c * N + a * 128:c * N + (a + 1) * 128],
                                                   src[:, a, c * 128:(c + 1) * 128], ident[:, :])
                last.then_inc(s_bank_full, 1)

            def columns(t, stage, use, w, xT, blocks):
                to = take(t, stage, use)
                for i, blk in enumerate(blocks):
                    n = 0
                    for c in range(CB):
                        for a, b in PARTS:
                            last = nc.tensor.matmul(to[:, i * N:(i + 1) * N], w[a][:, c, blk * 128:(blk + 1) * 128],
                                                    xT[:, b, c, :], start=(n == 0), stop=(n == 3 * CB - 1))
                            n += 1
                last.then_inc(s_bank_full, 1)

            def tokens(to, xT, w, c0, blocks, at, a):
                n = 0
                for c in range(blocks):
                    for i, j in PARTS:
                        last = nc.tensor.matmul(to[:, at:at + H], xT[:, i, c, a * 128:(a + 1) * 128],
                                                w[j][:, c, c0:c0 + H], start=(n == 0), stop=(n == 3 * blocks - 1))
                        n += 1
                return last

            def project(t, stage, wq, xq, wkv, k_blk, xkv):
                columns(t, stage, 0, wq, xq, (0, 1))
                columns(t, stage, 1, wkv, xkv, (k_blk, k_blk + 1))
                to = take(t, stage, 2)
                for a in range(NB):
                    last = tokens(to, xkv, wkv, (k_blk + 2) * 128, CB, a * H, a)
                last.then_inc(s_bank_full, 1)

            def heads(t, scan, attend):
                if scan:
                    s1 = scan[-1]
                    scans = before(SCANS, t, scan)
                    loads = before(LOADS_X if s1 == "x" else LOADS_Y, t, scan)
                    pe.wait_ge(s_load[s1], loads * 16)
                if attend:
                    s2 = attend[-1]
                    scores = before(ATTENDS, t, attend)
                    groups = before(GROUPS, t, attend)
                    halves = before(HALVES, t, attend)
                    pe.wait_ge(s_row, before(ROWS, t, attend) * 16)

                def values(grp):
                    half, g = divmod(grp, 2)
                    pe.wait_ge(s_exp, scores + 4 * grp + 4)
                    if g == 0:
                        wait(pe, s_pv_read, halves + half - 1)
                    for kb in range(NB):
                        for j in range(4):
                            head = head_of(half, g, j)
                            last = nc.tensor.matmul(
                                pv_bank[half][32 * j:32 * j + 32, g * N:(g + 1) * N], V[s2][:, kb, head, :],
                                P[:, (4 * grp + j) % 8, kb, :], start=(kb == 0), stop=(kb == NB - 1))
                    last.then_inc(s_pv, 1)

                for s in range(NH + 2):
                    if s < NH:
                        p, par = divmod(s, 2)
                        if scan:
                            wait(pe, s_scan_done, scans + s - 1)
                            for a in range(NB):
                                last = nc.tensor.matmul(
                                    scan_bank[s % 2][:, a * N:(a + 1) * N],
                                    QS[s1][64 * par:64 * par + 3 * HD, p, a * 128:(a + 1) * 128],
                                    KS[s1][64 * par:64 * par + 3 * HD, p, :], start=True, stop=True)
                            last.then_inc(s_scan_full, 1)
                        if attend:
                            wait(pe, s_exp, scores + s - 1)
                            for kb in range(NB):
                                last = nc.tensor.matmul(
                                    score_bank[s % 2][:, kb * N:(kb + 1) * N],
                                    KS[s2][64 * par:64 * par + 3 * HD + 2, p, kb * 128:(kb + 1) * 128],
                                    QS[s2][64 * par:64 * par + 3 * HD + 2, p, :], start=True, stop=True)
                            last.then_inc(s_score_full, 1)
                    if attend and s >= 5 and (s - 5) % 4 == 0:
                        values((s - 5) // 4)

            def maxima(t, stage):
                to = take(t, stage, 0)
                pe.wait_ge(s_max, before({"max_x": 1, "max_y": 1}, t, stage) + 1)
                for a in range(NB):
                    last = nc.tensor.transpose(to[0:2 * NH, a * 128:(a + 1) * 128],
                                               MH[:, a, :, :].rearrange("p a b -> p (a b)").bitcast(fp32), ident[:, :])
                last.then_inc(s_bank_full, 1)

            def outputs(t, stage, w, attend):
                to = take(t, stage, 0)
                pe.wait_ge(s_OT, before(HALVES, t, stage))
                for a in range(NB):
                    last = tokens(to, OT, w, 0, 2, a * H, a)
                last.then_inc(s_bank_full, 1)

            def step(t, has):
                if isinstance(t, int) and t == 0:
                    pe.wait_ge(s_weight_lo, 4)
                if has("norm_y"):
                    pe.wait_ge(s_xn_y, t)
                    transposes(t, "norm_y", 0, xn_a)
                    pe.wait_ge(s_xn_c, t)
                    transposes(t, "norm_y", 1, xn_b)
                heads(t, has("scan_x") and "scan_x", has("attend_y") and "attend_y")
                if has("project_y"):
                    pe.wait_ge(s_bank_done, before(BANK_USES, t, "norm_y") + 2)
                    project(t, "project_y", w_qc, xT_y, w_kvc, 0, xT_c)
                if has("max_x"):
                    maxima(t, "max_x")
                if has("out_y"):
                    outputs(t, "out_y", w_cproj, "attend_y")
                    pe.wait_ge(s_xn_m, t - 1)
                    transposes(t, "out_y", 1, xn_a)
                if has("norm_x"):
                    pe.wait_ge(s_xn_x, t + 2)
                    transposes(t, "norm_x", 0, xn_b)
                if has("mlp_up"):
                    pe.wait_ge(s_bank_done, before(BANK_USES, t, "out_y") + 2)
                    for u in range(FB // 2):
                        columns(t, "mlp_up", u, w_mlp1, xT_c, (2 * u, 2 * u + 1))
                heads(t, has("scan_y") and "scan_y", has("attend_x") and "attend_x")
                if has("project_x"):
                    if isinstance(t, int) and t == FIRST:
                        pe.wait_ge(s_weight_lo, 1)
                    pe.wait_ge(s_bank_done, before(BANK_USES, t, "norm_x") + 1)
                    project(t, "project_x", w_qkv, xT_x, w_qkv, 2, xT_x)
                if has("max_y"):
                    maxima(t, "max_y")
                if has("out_x"):
                    outputs(t, "out_x", w_proj, "attend_x")
                if has("mlp_down"):
                    pe.wait_ge(s_hidden_lo, (t - 2) * 4 + 4)
                    for a in range(NB):
                        to = take(t, "mlp_down", a)
                        tokens(to, HH, w_mlp2, 0, FB, 0, a).then_inc(s_bank_full, 1)

            steps(pe, step)

        @block.scalar
        def _(act):
            act.wait_ge(s_small, 16 * 8)
            nc.scalar.activation(cond_sb[:, 1, :], cond_sb[:, 0, :], ACT.Exp, scale=-1.0).then_inc(s_exp0, 1)

            def split_weights(i):
                act.wait_ge(s_weight[i], 16 * (2, 33, 1, 1)[i])
                src = P[:, :, :, :].rearrange("p a b c -> p (a b c)")[:, (i % 2) * 2048:(i % 2 + 1) * 2048]
                nc.scalar.activation(WT[:, HI, i * 2048:(i + 1) * 2048], src, ACT.Copy).then_inc(s_weight_hi, 1)

            split_weights(0)

            def full(t, stage, use):
                act.wait_ge(s_bank_full, before(BANK_USES, t, stage) + use + 1)
                return bank[bank_of(t, stage, use)]

            def modulated(t, stage, use, mod, loaded, count):
                act.wait_ge(loaded, count)
                src = full(t, stage, use)
                for c in range(CB):
                    last = nc.scalar.activation(xm[:, c, :], src[:, c * N:(c + 1) * N], ACT.Identity,
                                                bias=mod[:, c:c + 1], scale=mod[:, 2 + c:3 + c])
                last.then_inc(s_bank_hi, 1)

            def project(t, stage, cols):
                wait(act, s_store, before(STORES, t, stage) * 16)
                for use, dst in enumerate((SQ, SK)):
                    src = full(t, stage, use)
                    for i in range(2):
                        last = nc.scalar.activation(dst[:, HI, i, :], src[:, i * N:(i + 1) * N], ACT.Identity,
                                                    bias=bias_cols[:, cols[use] + i:cols[use] + i + 1])
                    last.then_inc(s_bank_hi, 1)

            def exponentials(t, stage):
                scores = before(ATTENDS, t, stage)
                groups = before(GROUPS, t, stage)
                for s in range(NH):
                    act.wait_ge(s_score_full, scores + s + 1)
                    if s % 4 == 0:
                        wait(act, s_pv, groups + s // 4 - 1)
                    nc.scalar.activation(P[:, s % 8, :, :].rearrange("p a n -> p (a n)"), score_bank[s % 2][:, :],
                                         ACT.Exp, scale=SCALE).then_inc(s_exp, 1)

            def step(t, has):
                if isinstance(t, int) and t == 0:
                    for i in range(1, 4):
                        split_weights(i)
                    act.wait_ge(s_weight_lo, 4)
                if has("norm_y"):
                    for use, dst in enumerate((xT_y, xT_c)):
                        src = full(t, "norm_y", use)
                        nc.scalar.activation(dst[:, HI, :, :].rearrange("p c n -> p (c n)"), src[:, :],
                                             ACT.Copy).then_inc(s_bank_hi, 1)
                if has("attend_y"):
                    exponentials(t, "attend_y")
                if has("project_y"):
                    project(t, "project_y", (QCC, KVCC))
                if has("out_y"):
                    modulated(t, "out_y", 1, mod_m, s_modm, (t - 2) * 16 + 16)
                if has("norm_x"):
                    modulated(t, "norm_x", 0, mod_x, s_modx, (t + 1) * 16 + 16)
                if has("mlp_up"):
                    for u in range(FB // 2):
                        src = full(t, "mlp_up", u)
                        wait(act, s_hidden_lo, (t - 2) * 4 + u - 1)
                        for i in range(2):
                            col = MLPC + 2 * u + i
                            last = nc.scalar.activation(HF[:, u % 2, i, :], src[:, i * N:(i + 1) * N],
                                                        ACT.Gelu_apprx_tanh, bias=bias_cols[:, col:col + 1])
                        last.then_inc(s_bank_hi, 1)
                if has("attend_x"):
                    exponentials(t, "attend_x")
                if has("project_x"):
                    project(t, "project_x", (QKVC, QKVC + 2))

            steps(act, step)

        @block.vector
        def _(dve):
            nc.vector.memset(QS["x"][:, :, :].bitcast(fp32), 0.0)
            nc.vector.memset(QS["y"][:, :, :].bitcast(fp32), 0.0)
            dve.wait_ge(s_exp0, 1)
            nc.vector.tensor_scalar_add(cond_sb[:, 2, :], cond_sb[:, 1, :], 1.0).then_inc(s_silu_part, 1)
            dve.wait_ge(s_silu_part, 1)
            nc.vector.reciprocal(cond_sb[:, 1, :], cond_sb[:, 2, :]).then_inc(s_silu_part, 1)
            dve.wait_ge(s_silu_part, 2)
            nc.vector.tensor_tensor(cond_sb[:, 2, :], cond_sb[:, 1, :], cond_sb[:, 0, :], ALU.mult).then_inc(s_silu, 1)
            dve.wait_ge(s_startT, 1)
            nc.vector.tensor_copy(bias_cols[:, :], scan_bank[0][:, 0:32])
            nc.vector.tensor_copy(silu_T[:, :, :].rearrange("p c b -> p (c b)"),
                                  scan_bank[1][:, 0:CB * B]).then_inc(s_startC, 1)
            dve.wait_ge(s_startC, 1)
            dve.wait_ge(s_mod, 1)
            for k, blk in enumerate((0, 1, 2, 3, 6, 7, 8, 9)):
                last = nc.vector.tensor_scalar(mod_all[:, :, k], score_bank[0][:, k * B:(k + 1) * B],
                                               bias_cols[:, blk:blk + 1], float(k % 4 // 2), ALU.add, ALU.add)
            last.then_inc(s_modC, 1)
            dve.wait_ge(s_mod, 2)
            dve.wait_ge(s_small, 16 * 8)
            nc.vector.tensor_tensor(gate_all, score_bank[1][0:B, :], gate_bias, ALU.add).then_inc(s_modC, 1)

            def split_weights(i):
                dve.wait_ge(s_weight_hi, i + 1)
                src = P[:, :, :, :].rearrange("p a b c -> p (a b c)")[:, (i % 2) * 2048:(i % 2 + 1) * 2048]
                nc.vector.tensor_tensor(WT[:, LO, i * 2048:(i + 1) * 2048], src,
                                        WT[:, HI, i * 2048:(i + 1) * 2048].bitcast(fp32),
                                        ALU.subtract).then_inc(s_weight_lo, 1)

            split_weights(0)
            dve.wait_ge(s_const, 16 * 5)
            dve.wait_ge(s_ident, 3)

            class Chain:
                def __init__(self, t, stage):
                    self.base, self.n, self.most = before(LINKS, t, stage), 0, LINKS[stage]

                def __call__(self, instruction):
                    self.n += 1
                    instruction.then_inc(s_link, 1)
                    dve.wait_ge(s_link, self.base + self.n)

                def end(self):
                    assert self.n == self.most, (self.n, self.most)

            def full(t, stage, use):
                dve.wait_ge(s_bank_full, before(BANK_USES, t, stage) + use + 1)
                return bank[bank_of(t, stage, use)]

            def hi_done(t, stage, use):
                dve.wait_ge(s_bank_hi, before(ACT_USES, t, stage) + use + 1)

            def norm(t, stage, link, pairs):
                k = 0
                for src, _, _ in pairs:
                    for a in range(NB):
                        last = nc.vector.bn_stats(stats[:, k, :], src[:, a, :])
                        k += 1
                link(last)
                nc.vector.memset(spare[:, :], 0.0)
                for i in range(k):
                    last = nc.vector.bn_aggr(mv[:, i, :], stats[:, i, :])
                last.then_inc(s_mv, 1)
                dve.wait_ge(s_mv, before(NORMS, t, stage) + 1)
                dve.wait_ge(s_rstd, before(NORMS, t, stage) + 1)
                k = 0
                for src, dst, ready in pairs:
                    for a in range(NB):
                        last = nc.vector.tensor_scalar(dst[:, a, :], src[:, a, :], mv[:, k, 0:1], rstd[:, k:k + 1],
                                                       ALU.subtract, ALU.mult)
                        k += 1
                    last.then_inc(ready, 1)

            def split_modulated(t, stage, use, act_use, link, xT):
                hi_done(t, stage, act_use)
                link(nc.vector.tensor_copy(xT[:, HI, :, :], xm[:, :, :]))
                nc.vector.tensor_tensor(xT[:, LO, :, :], xm[:, :, :], xT[:, HI, :, :].bitcast(fp32),
                                        ALU.subtract).then_inc(s_bank_done, 1)

            def project(t, stage, s, cols):
                for use, dst in enumerate((SQ, SK)):
                    src = full(t, stage, use)
                    hi_done(t, stage, use)
                    for i in range(2):
                        col = cols[use] + i
                        last = nc.vector.scalar_tensor_tensor(
                            out=dst[:, LO, i, :], in0=src[:, i * N:(i + 1) * N], scalar=bias_cols[:, col:col + 1],
                            in1=dst[:, HI, i, :].bitcast(fp32), op0=ALU.add, op1=ALU.subtract)
                    last.then_inc(s_bank_done, 1)
                src = full(t, stage, 2)
                for a in range(NB):
                    last = nc.vector.tensor_tensor(
                        V[s][:, a, :, 0:HD], src[:, a * H:(a + 1) * H].rearrange("p (h d) -> p h d", d=HD),
                        bc_v[s][:, :].rearrange("p (h d) -> p h d", d=HD), ALU.add)
                last.then_inc(s_bank_done, 1)

            def normalise(t, stage, half, link):
                read = before(HALVES, t, stage) + half
                dve.wait_ge(s_pv, before(GROUPS, t, stage) + 2 * half + 2)
                nc.vector.transpose(PT[:, :, :, :].rearrange("p a b c -> p (a b c)"), pv_bank[half][:, :])\
                    .then_inc(s_pv_read, 1)
                dve.wait_ge(s_pv_read, read + 1)
                link(nc.vector.reciprocal(rsum[:, :, :], PT[:, :, :, HD]))
                link(nc.vector.tensor_tensor(PN[:, :, :, :].rearrange("p b a d -> p a b d"), PT[:, :, :, 0:HD],
                                             rsum[:, :, :].unsqueeze(3).to_broadcast([128, 2, 8, HD]), ALU.mult))
                link(nc.vector.transpose(PO[:, :], PN[:, :, :, :].rearrange("p a b c -> p (a b c)")))
                link(nc.vector.tensor_copy(OT[:, HI, half, :], PO[:, :]))
                nc.vector.tensor_tensor(OT[:, LO, half, :], PO[:, :], OT[:, HI, half, :].bitcast(fp32),
                                        ALU.subtract).then_inc(s_OT, 1)

            def heads(t, scan, attend):
                if attend:
                    link = Chain(t, attend)
                for s in range(NH):
                    if scan:
                        p, par = divmod(s, 2)
                        dve.wait_ge(s_scan_full, before(SCANS, t, scan) + s + 1)
                        nc.vector.tensor_reduce(MX[:, :, par, p], scan_bank[s % 2][:, :].rearrange("p (a n) -> p a n", a=NB),
                                                AXIS.X, ALU.max, negate=True).then_inc(s_scan_done, 1)
                    if attend and s == 12:
                        normalise(t, attend, 0, link)
                if attend:
                    normalise(t, attend, 1, link)
                    link.end()

            def split_maxima(t, stage, scan):
                link = Chain(t, stage)
                dve.wait_ge(s_scan_done, before(SCANS, t, stage))
                flat = MX[:, :, :, :].rearrange("p a b c -> p a (b c)")
                link(nc.vector.tensor_copy(MH[:, :, HI, :], flat))
                nc.vector.tensor_tensor(MH[:, :, LO, :], flat, MH[:, :, HI, :].bitcast(fp32),
                                        ALU.subtract).then_inc(s_max, 1)
                link.end()

            def copy_maxima(t, stage):
                src = full(t, stage, 0)
                wait(dve, s_row, before(ROWS, t, stage) * 16)
                nc.vector.tensor_copy(MT[:, :], src[0:2 * NH, 0:N]).then_inc(s_bank_done, 1)

            def step(t, has):
                if isinstance(t, int) and t == 0:
                    for i in range(1, 4):
                        split_weights(i)
                if has("norm_y"):
                    link = Chain(t, "norm_y")
                    dve.wait_ge(s_c, t * 16)
                    dve.wait_ge(s_x1, t)
                    norm(t, "norm_y", link, ((x1, xn_a, s_xn_y), (c_in, xn_b, s_xn_c)))
                    link.end()
                    for use, xT in enumerate((xT_y, xT_c)):
                        src = full(t, "norm_y", use)
                        hi_done(t, "norm_y", use)
                        nc.vector.tensor_tensor(xT[:, LO, :, :].rearrange("p c n -> p (c n)"), src[:, :],
                                                xT[:, HI, :, :].rearrange("p c n -> p (c n)").bitcast(fp32),
                                                ALU.subtract).then_inc(s_bank_done, 1)
                heads(t, has("scan_x") and "scan_x", has("attend_y") and "attend_y")
                if has("max_x"):
                    split_maxima(t, "max_x", "scan_x")
                if has("project_y"):
                    project(t, "project_y", "y", (QCC, KVCC))
                if has("max_x"):
                    copy_maxima(t, "max_x")
                if has("out_y"):
                    link = Chain(t, "out_y")
                    src = full(t, "out_y", 0)
                    dve.wait_ge(s_x1_bias, t - 1)
                    wait(dve, s_x2_bias, t - 2)
                    nc.vector.tensor_tensor(x2[:, :, :].rearrange("p a c -> p (a c)"), src[:, :],
                                            x1_bias[:, :, :].rearrange("p a c -> p (a c)"),
                                            ALU.add).then_inc(s_bank_done, 1)
                    dve.wait_ge(s_bank_done, before(BANK_USES, t, "out_y") + 1)
                    norm(t, "out_y", link, ((x2, xn_a, s_xn_m),))
                    split_modulated(t, "out_y", 1, 0, link, xT_c)
                    link.end()
                if has("norm_x"):
                    link = Chain(t, "norm_x")
                    dve.wait_ge(s_x, (t + 1) * 16 + 16)
                    norm(t, "norm_x", link, ((x_in, xn_b, s_xn_x),))
                    split_modulated(t, "norm_x", 0, 0, link, xT_x)
                    link.end()
                if has("mlp_up"):
                    for u in range(FB // 2):
                        hi_done(t, "mlp_up", u)
                        nc.vector.tensor_copy(HH[:, HI, 2 * u:2 * u + 2, :],
                                              HF[:, u % 2, :, :]).then_inc(s_bank_done, 1)
                heads(t, has("scan_y") and "scan_y", has("attend_x") and "attend_x")
                if has("max_y"):
                    split_maxima(t, "max_y", "scan_y")
                if has("project_x"):
                    project(t, "project_x", "x", (QKVC, QKVC + 2))
                if has("max_y"):
                    copy_maxima(t, "max_y")
                if has("out_x"):
                    src = full(t, "out_x", 0)
                    for a in range(NB):
                        last = nc.vector.tensor_tensor(gated[:, a, :], src[:, a * H:(a + 1) * H], gate_a[:, :], ALU.mult)
                    last.then_inc(s_bank_done, 1)
                    dve.wait_ge(s_bank_done, before(BANK_USES, t, "out_x") + 1)
                    dve.wait_ge(s_x_bias, t + 1)
                    wait(dve, s_x1_bias, t)
                    nc.vector.tensor_tensor(x1[:, :, :], gated[:, :, :], x_bias[:, :, :], ALU.add).then_inc(s_x1, 1)
                if has("mlp_down"):
                    dve.wait_ge(s_x2_bias, t - 1)
                    wait(dve, s_out, (t - 2) * 16)
                    for a in range(NB):
                        src = full(t, "mlp_down", a)
                        nc.vector.tensor_tensor(y[:, a, :], src[:, 0:H], gate_m[:, :], ALU.mult).then_inc(s_bank_done, 1)
                        dve.wait_ge(s_bank_done, before(BANK_USES, t, "mlp_down") + a + 1)
                        nc.vector.tensor_tensor(y[:, a, :], y[:, a, :], x2_bias[:, a, :], ALU.add).then_inc(s_y, 1)

            steps(dve, step)


_INS = ["x", "cond_1024", "ctx_1024"] + ["L0_xcond_" + n for n in (
    "W_mod", "b_mod", "W_qkv", "b_qkv", "W_proj", "b_proj", "W_qc", "b_qc", "W_kvc", "b_kvc",
    "W_cproj", "b_cproj", "W_mlp1", "b_mlp1", "W_mlp2", "b_mlp2")]


def kernel(**inputs):
    import numpy as np
    import concourse.bacc as bacc
    from concourse.bass_utils import run_bass_kernel_spmd

    nc = bacc.Bacc("TRN2", target_bir_lowering=False, num_devices=1)
    arrays, args = {}, []
    for name in _INS:
        a = np.ascontiguousarray(inputs[name])
        arrays["in_" + name] = a
        args.append(nc.dram_tensor("in_" + name, a.shape, mybir.dt.from_np(a.dtype), kind="ExternalInput").ap())
    args.append(nc.dram_tensor("out_x", (B, N, H), fp32, kind="ExternalOutput").ap())
    build(nc, *args)
    r = run_bass_kernel_spmd(nc, [arrays], core_ids=[0])
    return r.results[0]["out_x"]
```

```python
import concourse.bass as bass
from concourse import mybir
from contextlib import ExitStack

fp32 = mybir.dt.float32
f32r = mybir.dt.float32r
ALU = mybir.AluOpType
ACT = mybir.ActivationFunctionType
AXIS = mybir.AxisListType

B, N, H, NH, MLP = 16, 256, 256, 16, 1024
HD = H // NH
CB = H // 128
NB = N // 128
FB = MLP // 128
PAIRS = NH // 2
EPS = 1e-6
SCALE = HD ** -0.5
HI, LO = 0, 1

TAIL = NH
PLAN = {
    "A": [("scan_x", 0, 0), ("attend_y", -2, 0),
          ("mlp_up", -3, 1),
          ("out_x", -1, 2),
          ("stats_y", -1, 3), ("apply_y", -1, 4),
          ("T_y", -1, 5), ("T_c", -1, 5),
          ("q_y", -1, 7), ("k_y", -1, 8),
          ("split_x0", 0, 8), ("max_x0", 0, 9),
          ("v_y", -1, TAIL), ("split_x1", 0, TAIL), ("max_x1", 0, TAIL)],
    "B": [("scan_y", -1, 0), ("attend_x", 0, 0),
          ("stats_x", 1, 0), ("apply_x", 1, 1),
          ("down0", -3, 1),
          ("T_x", 1, 2),
          ("down1", -3, 3),
          ("out_y", -2, 4),
          ("stats_m", -2, 5), ("apply_m", -2, 6), ("T_m", -2, 7),
          ("q_x", 1, 8), ("k_x", 1, 9),
          ("split_y0", -1, 9), ("max_y0", -1, 10),
          ("v_x", 1, TAIL), ("split_y1", -1, TAIL), ("max_y1", -1, TAIL)],
}
STAGES = [(name, shift) for section in "AB" for name, shift, _ in PLAN[section]]
RANK = {name: i for i, (name, _) in enumerate(STAGES)}
SHIFT = dict(STAGES)
FIRST, LAST = -1, B + 2
LOOP = (4, B - 1)

BANK_USES = {n: 1 for n in ("out_x", "T_y", "T_c", "q_y", "k_y", "max_x0", "v_y", "max_x1", "down0", "T_x", "down1",
                            "out_y", "T_m", "q_x", "k_x", "max_y0", "v_x", "max_y1")} | {"mlp_up": FB // 2}
ACT_USES = {n: 1 for n in ("T_y", "T_c", "q_y", "k_y", "T_x", "T_m", "q_x", "k_x")} | {"mlp_up": FB // 2}
SCANS = {"scan_x": NH, "scan_y": NH}
ATTENDS = {"attend_x": NH, "attend_y": NH}
GROUPS = {"attend_x": 4, "attend_y": 4}
HALVES = {"attend_x": 2, "attend_y": 2}
NORMS = {"stats_y": 1, "stats_m": 1, "stats_x": 1}
LOADS = {"x": {"q_x": 12}, "y": {"q_y": 12}}
MAXIMA = {"split_x0": 1, "split_x1": 1, "split_y0": 1, "split_y1": 1}
ROWS = [{"max_x0": 2, "max_y0": 2}, {"max_x1": 2, "max_y1": 2}]
LINKS = {n: 1 for n in ("stats_y", "stats_x", "stats_m", "T_x", "T_m", *MAXIMA)}
POOL_LINKS = {"stats_y": 2}


def build(nc, x, cond, ctx_in, W_mod, b_mod, W_qkv, b_qkv, W_proj, b_proj, W_qc, b_qc, W_kvc, b_kvc,
          W_cproj, b_cproj, W_mlp1, b_mlp1, W_mlp2, b_mlp2, out):
    def before(per, t, stage):
        def at(step, clamp):
            total = 0
            for name, n in per.items():
                ran = step + SHIFT[name] + (1 if RANK[name] < RANK[stage] else 0)
                total += n * (min(max(ran, 0), B) if clamp else ran)
            return total
        if isinstance(t, int):
            return at(t, True)
        slope = at(1, False) - at(0, False)
        base = at(0, False)
        return t * slope + base if slope else base

    def bank_of(t, stage, use):
        return (before(BANK_USES, t if isinstance(t, int) else LOOP[0], stage) + use) % 2

    def wait(eng, sem, value):
        if not isinstance(value, int) or value > 0:
            eng.wait_ge(sem, value)

    def head_of(half, g, j):
        return (2 * (2 * half + g) + j // 2) + PAIRS * (j % 2)

    es = ExitStack()
    with es:
        def sb(name, shape, dt=fp32):
            return es.enter_context(nc.sbuf_tensor(name, shape, dt))

        def sem(name):
            return es.enter_context(nc.semaphore(name))

        def dram(name, shape, dt=fp32):
            return nc.dram_tensor(name, shape, dt, kind="Internal").ap()

        WT = sb("WT", [128, 2, 4 * 2048], f32r)

        def weight(start, blocks, cols):
            return [WT[:, part, start:start + blocks * cols].rearrange("p (c n) -> p c n", c=blocks)
                    for part in (HI, LO)]

        w_qkv = weight(0, CB, 3 * H)
        w_qc = weight(1536, CB, H)
        w_kvc = weight(2048, CB, 2 * H)
        w_proj = weight(3072, 2, H)
        w_cproj = weight(3584, 2, H)
        w_mlp1 = weight(4096, CB, MLP)
        w_mlp2 = weight(6144, FB, H)

        QS = {s: sb(f"QS_{s}", [128, PAIRS, N], f32r) for s in "xy"}
        KS = {s: sb(f"KS_{s}", [128, PAIRS, N], f32r) for s in "xy"}
        V = {s: sb(f"V_{s}", [128, NB, NH, 32]) for s in "xy"}
        P = sb("P", [128, 8, NB, N])
        SQ = sb("SQ", [128, 2, 2, N], f32r)
        SK = sb("SK", [128, 2, 2, N], f32r)
        xT_x = sb("xT_x", [128, 2, CB, N], f32r)
        xT_y = sb("xT_y", [128, 2, CB, N], f32r)
        xT_c = sb("xT_c", [128, 2, CB, N], f32r)
        xT_m = sb("xT_m", [128, 2, CB, N], f32r)
        HH = sb("HH", [128, 2, FB, N], f32r)
        HF = sb("HF", [128, 2, 2, N])
        xn_a = sb("xn_a", [128, NB, H])
        xn_b = sb("xn_b", [128, NB, H])
        x_in = sb("x_in", [128, NB, H])
        c_in = sb("c_in", [128, NB, H])
        x1 = sb("x1", [128, NB, H])
        x1_bias = sb("x1_bias", [128, NB, H])
        x2 = sb("x2", [128, NB, H])
        x2_bias = sb("x2_bias", [128, NB, H])
        x_bias = sb("x_bias", [128, NB, H])
        y = sb("y", [128, NB, H])
        xm = sb("xm", [128, CB, N])
        gated = xm
        PT = sb("PT", [128, 2, 8, 32])
        PN = sb("PN", [128, 8, 2, HD])
        PO = sb("PO", [128, N])
        OT = sb("OT", [128, 2, 2, N], f32r)
        rsum = sb("rsum", [128, 2, 8])
        MX = sb("MX", [128, NB, 2, 2, PAIRS // 2])
        MH = sb("MH", [128, 2, NB, 2, 2, PAIRS // 2], f32r)
        MT = [sb(f"MT{i}", [NH, N], f32r) for i in range(2)]
        stats = sb("stats", [128, 4, 6])
        mv = sb("mv", [128, 4, 2])
        rstd = sb("rstd", [128, 4])
        var_eps = sb("var_eps", [128, 4])
        minus_half = sb("minus_half", [128, 4])
        eps = sb("eps", [128, 4])
        spare = sb("spare", [128, 1])
        ident = sb("ident", [128, 128])
        bias_cols = sb("bias_cols", [128, 64])
        bc_v = {"x": sb("bc_v_x", [128, H]), "y": sb("bc_v_y", [128, H])}
        bc_proj = sb("bc_proj", [128, H])
        bc_cproj = sb("bc_cproj", [128, H])
        bc_mlp2 = sb("bc_mlp2", [128, H])
        gb_a = sb("gb_a", [128, H])
        gb_m = sb("gb_m", [128, H])
        gate_a = sb("gate_a", [128, H])
        gate_m = sb("gate_m", [128, H])
        mod_x = sb("mod_x", [128, 4])
        mod_m = sb("mod_m", [128, 4])
        bias_rows = xn_a[0:32, 0, 0:128]
        turned_rows = xn_a[0:32, 1, 0:128]
        cond_sb = HF[0:B, :, :, :].rearrange("p a b c -> p (a b) c")
        silu_T = sb("silu_T", [128, CB, B])
        mod_all = sb("mod_all", [128, B, 8])
        gate_bias = x2_bias[0:B, :, :].rearrange("p a c -> p (a c)")
        gate_all = x2[0:B, :, :].rearrange("p a c -> p (a c)")

        d_mod = dram("d_mod", (B, 128, 8))
        d_gate = dram("d_gate", (B, 2 * H))
        scan_bank = [es.enter_context(nc.psum_tensor(f"scan{i}", [128, 512], fp32)) for i in range(2)]
        score_bank = [es.enter_context(nc.psum_tensor(f"score{i}", [128, 512], fp32)) for i in range(2)]
        pv_bank = [es.enter_context(nc.psum_tensor(f"pv{i}", [128, 512], fp32)) for i in range(2)]
        bank = [es.enter_context(nc.psum_tensor(f"bank{i}", [128, 512], fp32)) for i in range(2)]

        s_ident = sem("s_ident")
        s_const = sem("s_const")
        s_small = sem("s_small")
        s_wmod = sem("s_wmod")
        s_weight = [sem(f"s_weight{i}") for i in range(4)]
        s_weight_hi = sem("s_weight_hi")
        s_weight_lo = sem("s_weight_lo")
        s_silu = sem("s_silu")
        s_silu_part = sem("s_silu_part")
        s_bias_rows = sem("s_bias_rows")
        s_exp0 = sem("s_exp0")
        s_startT = sem("s_startT")
        s_startC = sem("s_startC")
        s_mod = sem("s_mod")
        s_modC = sem("s_modC")
        s_modD = sem("s_modD")
        s_x = sem("s_x")
        s_modx = sem("s_modx")
        s_c = sem("s_c")
        s_gate_a = sem("s_gate_a")
        s_gate_m = sem("s_gate_m")
        s_modm = sem("s_modm")
        s_bank_full = sem("s_bank_full")
        s_bank_hi = sem("s_bank_hi")
        s_bank_done = sem("s_bank_done")
        s_scan_full = sem("s_scan_full")
        s_scan_done = sem("s_scan_done")
        s_score_full = sem("s_score_full")
        s_exp = sem("s_exp")
        s_pv = sem("s_pv")
        s_pv_read = sem("s_pv_read")
        s_OT = sem("s_OT")
        s_max = sem("s_max")
        s_row = [sem(f"s_row{i}") for i in range(2)]
        s_load = {s: [sem(f"s_load_{s}{i}") for i in range(2)] for s in "xy"}
        s_mv = sem("s_mv")
        s_eps = sem("s_eps")
        s_rstd = sem("s_rstd")
        s_xn_y, s_xn_c, s_xn_m, s_xn_x = sem("s_xn_y"), sem("s_xn_c"), sem("s_xn_m"), sem("s_xn_x")
        s_gb_a, s_gb_m = sem("s_gb_a"), sem("s_gb_m")
        s_x_bias = sem("s_x_bias")
        s_x1 = sem("s_x1")
        s_x1_bias = sem("s_x1_bias")
        s_x2_bias = sem("s_x2_bias")
        s_hidden_lo = sem("s_hidden_lo")
        s_y = sem("s_y")
        s_out = sem("s_out")
        s_link = sem("s_link")
        s_link_pv = sem("s_link_pv")
        s_pool = sem("s_pool")

        def weight_views(i, part):
            src = P[:, :, :, :].rearrange("p a b c -> p (a b c)")[:, (i % 2) * 2048:(i % 2 + 1) * 2048]
            dst = WT[:, part, i * 2048:(i + 1) * 2048]

            def turned(lo, hi):
                return (dst[:, lo:hi].rearrange("p (b d h) -> p b h d", d=HD, h=PAIRS // 2),
                        src[:, lo:hi].rearrange("p (b h d) -> p b h d", d=HD, h=PAIRS // 2))

            def plain(lo, hi):
                return dst[:, lo:hi], src[:, lo:hi]

            if i == 0:
                return [turned(0, 2 * H), plain(2 * H, 3 * H), turned(3 * H, 5 * H), plain(5 * H, 6 * H),
                        turned(6 * H, 8 * H)]
            if i == 1:
                return [turned(0, H), plain(H, 2 * H), turned(2 * H, 3 * H), plain(3 * H, 8 * H)]
            return [plain(0, 2048)]

        block = es.enter_context(nc.Block())

        def steps(eng, step):
            for t in range(FIRST, LOOP[0]):
                yield_step(step, t)
            with eng.Fori(LOOP[0], LOOP[1]) as t:
                step(t, lambda name: True)
            for t in range(LOOP[1], LAST + 1):
                yield_step(step, t)

        def yield_step(step, t):
            step(t, lambda name: 0 <= t + SHIFT[name] < B)

        def section(letter, t, has, slot, tasks):
            for s in range(TAIL + 1):
                if s < TAIL:
                    slot(s)
                for name, _, at in PLAN[letter]:
                    if at == s and name in tasks and has(name):
                        tasks[name](t)

        MODC, QKVC, QCC, KVCC, MLPC = 0, 12, 18, 20, 24
        PARTS = ((HI, HI), (HI, LO), (LO, HI))

        @block.sync
        def _(sp):
            sp.dma_start(cond_sb[:, 0, :], cond).then_inc(s_small, 16)
            for start, src in ((MODC, b_mod), (QKVC, b_qkv), (QCC, b_qc), (KVCC, b_kvc), (MLPC, b_mlp1)):
                rows = src.rearrange("(k p) -> k p", p=128)
                sp.dma_start(bias_rows[start:start + rows.shape[0], :], rows).then_inc(s_small, 16)
            for i in range(2):
                sp.dma_start(gate_bias[:, i * H:(i + 1) * H],
                             b_mod[(3 * i + 2) * H:(3 * i + 3) * H].partition_broadcast(B)).then_inc(s_small, 16)
            stage_w = P[:, :, :, :].rearrange("p a b c -> p (a b c)")
            sp.dma_start(stage_w[:, 0:CB * 6 * H].rearrange("p (c n) -> p c n", c=CB),
                         W_mod.rearrange("(c p) n -> p c n", p=128)).then_inc(s_wmod, 16)
            for dst, src in ((bc_v["x"], b_qkv[2 * H:3 * H]), (bc_v["y"], b_kvc[H:2 * H]), (bc_proj, b_proj),
                             (bc_cproj, b_cproj), (bc_mlp2, b_mlp2)):
                sp.dma_start(dst[:, :], src.partition_broadcast(128)).then_inc(s_const, 16)

            def load_weights(i):
                if i < 2:
                    sp.wait_ge(s_mod, 2)
                else:
                    sp.wait_ge(s_weight_lo, i - 1)
                to = stage_w[:, (i % 2) * 2048:(i % 2 + 1) * 2048]
                if i == 0:
                    sp.dma_start(to[:, 0:1536].rearrange("p (c n) -> p c n", c=CB),
                                 W_qkv.rearrange("(c p) n -> p c n", p=128)).then_inc(s_weight[i], 16)
                    sp.dma_start(to[:, 1536:2048].rearrange("p (c n) -> p c n", c=CB),
                                 W_qc.rearrange("(c p) n -> p c n", p=128)).then_inc(s_weight[i], 16)
                elif i == 1:
                    sp.dma_start(to[:, 0:1024].rearrange("p (c n) -> p c n", c=CB),
                                 W_kvc.rearrange("(c p) n -> p c n", p=128)).then_inc(s_weight[i], 16)
                    for k, w in enumerate((W_proj, W_cproj)):
                        dst = to[:, 1024 + 512 * k:1536 + 512 * k].rearrange("p (c n) -> p c n", c=2)
                        for g in range(2):
                            for j in range(4):
                                row = 32 * j + HD * g
                                for half in range(2):
                                    head = head_of(half, g, j)
                                    sp.dma_start(dst[row:row + HD, half, :],
                                                 w[head * HD:(head + 1) * HD, :]).then_inc(s_weight[i], 16)
                elif i == 2:
                    sp.dma_start(to.rearrange("p (c n) -> p c n", c=CB),
                                 W_mlp1.rearrange("(c p) n -> p c n", p=128)).then_inc(s_weight[i], 16)
                else:
                    sp.dma_start(to.rearrange("p (c n) -> p c n", c=FB),
                                 W_mlp2.rearrange("(c p) n -> p c n", p=128)).then_inc(s_weight[i], 16)

            sp.wait_ge(s_modC, 1)
            sp.dma_start(d_mod.rearrange("b p k -> p b k"), mod_all[:, :, :]).then_inc(s_modD, 16)
            load_weights(0)
            sp.wait_ge(s_modC, 2)
            sp.dma_start(d_gate, gate_all).then_inc(s_modD, 16)
            sp.wait_ge(s_modD, 32)

            def stacks(t, s, half, attend, has):
                if half == 0:
                    sp.wait_ge(s_bank_done, before(BANK_USES, t, "k_" + s) + 1)
                else:
                    wait(sp, s_score_full, before(ATTENDS, t, attend) + (NH if has(attend) else 0))
                for src, dst, parts in ((SQ, QS[s], (HI, HI, LO)), (SK, KS[s], (HI, LO, HI))):
                    for par in range(2):
                        for c, part in enumerate(parts):
                            row = 64 * par + HD * c
                            sp.dma_start(dst[row:row + HD, 4 * half:4 * half + 4, :].bitcast(fp32),
                                         src[64 * half:64 * half + 64, part, par, :].bitcast(fp32))\
                                .then_inc(s_load[s][half], 16)

            def rows(t, s, half):
                sp.wait_ge(s_bank_done, before(BANK_USES, t, f"max_{s}{half}") + 1)
                for par in range(2):
                    row = 64 * par + 3 * HD
                    sp.dma_start(QS[s][row:row + 2, 4 * half:4 * half + 4, :].bitcast(fp32),
                                 MT[half][8 * par:8 * par + 8, :].bitcast(fp32)).then_inc(s_row[half], 16)

            def step(t, has):
                if has("down0"):
                    wait(sp, s_y, (t - 3) * 2)
                    sp.dma_start(gate_m[:, :], d_gate[t - 3, H:2 * H].partition_broadcast(128)).then_inc(s_gate_m, 16)
                if has("T_m"):
                    sp.dma_start(mod_m[:, :], d_mod[t - 2, :, 4:8]).then_inc(s_modm, 16)
                if has("scan_x"):
                    wait(sp, s_x1, t)
                    sp.dma_start(gate_a[:, :], d_gate[t, 0:H].partition_broadcast(128)).then_inc(s_gate_a, 16)
                if has("stats_x"):
                    wait(sp, s_x_bias, t + 1)
                    sp.dma_start(x_in[:, :, :], x[t + 1].rearrange("(a p) c -> p a c", p=128)).then_inc(s_x, 16)
                    sp.dma_start(mod_x[:, :], d_mod[t + 1, :, 0:4]).then_inc(s_modx, 16)
                if isinstance(t, int) and t == FIRST:
                    load_weights(1)
                    load_weights(2)
                for half in range(2):
                    if has("q_y"):
                        stacks(t, "y", half, "attend_y", has)
                    if has("scan_x"):
                        rows(t, "x", half)
                if isinstance(t, int) and t == 0:
                    load_weights(3)
                if has("scan_x"):
                    wait(sp, s_xn_c, t)
                    sp.dma_start(c_in[:, :, :], ctx_in[t].rearrange("(a p) c -> p a c", p=128)).then_inc(s_c, 16)
                if has("down1"):
                    sp.wait_ge(s_y, (t - 3) * 2 + 2)
                    sp.dma_start(out[t - 3].rearrange("(a p) c -> p a c", p=128), y[:, :, :]).then_inc(s_out, 16)
                for half in range(2):
                    if has("q_x"):
                        stacks(t, "x", half, "attend_x", has)
                    if has("scan_y"):
                        rows(t, "y", half)

            steps(sp, step)
            sp.wait_ge(s_out, 16 * B)

        @block.gpsimd
        def _(pool):
            nc.gpsimd.memset(ident[:, :], 0.0).then_inc(s_pool, 1)
            pool.wait_ge(s_pool, 1)
            nc.gpsimd.affine_select(out=ident[:, :], in_=ident[:, :], compare_op=ALU.not_equal, fill=1.0, base=0,
                                    pattern=[[-1, 128]], channel_multiplier=1).then_inc(s_ident, 1)
            nc.gpsimd.memset(V["x"][:, :, :, :], 1.0)
            nc.gpsimd.memset(V["y"][:, :, :, :], 1.0).then_inc(s_ident, 1)
            nc.gpsimd.memset(KS["x"][:, :, :].bitcast(fp32), 1.0)
            nc.gpsimd.memset(KS["y"][:, :, :].bitcast(fp32), 1.0).then_inc(s_ident, 1)
            nc.gpsimd.memset(eps[:, :], EPS)
            nc.gpsimd.memset(minus_half[:, :], -0.5).then_inc(s_ident, 1)
            pool.wait_ge(s_ident, 4)
            pool.wait_ge(s_const, 16 * 5)

            def deviation(t, stage, n):
                pool.wait_ge(s_mv, before(NORMS, t, stage) + 1)
                nc.gpsimd.tensor_tensor(var_eps[:, 0:n], mv[:, 0:n, 1], eps[:, 0:n], ALU.add).then_inc(s_eps, 1)
                pool.wait_ge(s_eps, before(NORMS, t, stage) + 1)
                nc.gpsimd.tensor_tensor(rstd[:, 0:n], var_eps[:, 0:n], minus_half[:, 0:n], ALU.pow).then_inc(s_rstd, 1)

            def step(t, has):
                if has("mlp_up"):
                    for u in range(FB // 2):
                        pool.wait_ge(s_bank_done, before(BANK_USES, t, "mlp_up") + u + 1)
                        nc.gpsimd.tensor_tensor(HH[:, LO, 2 * u:2 * u + 2, :], HF[:, u % 2, :, :],
                                                HH[:, HI, 2 * u:2 * u + 2, :].bitcast(fp32),
                                                ALU.subtract).then_inc(s_hidden_lo, 1)
                if has("stats_y"):
                    deviation(t, "stats_y", 4)
                if has("mlp_up"):
                    pool.wait_ge(s_gate_m, (t - 3) * 16 + 16)
                    nc.gpsimd.tensor_tensor(gb_m[:, :], gate_m[:, :], bc_mlp2[:, :], ALU.mult).then_inc(s_gb_m, 1)
                    pool.wait_ge(s_gb_m, t - 2)
                    for a in range(NB):
                        last = nc.gpsimd.tensor_tensor(x2_bias[:, a, :], x2[:, a, :], gb_m[:, :], ALU.add)
                    last.then_inc(s_x2_bias, 1)
                if has("scan_x"):
                    pool.wait_ge(s_gate_a, t * 16 + 16)
                    nc.gpsimd.tensor_tensor(gb_a[:, :], gate_a[:, :], bc_proj[:, :], ALU.mult).then_inc(s_gb_a, 1)
                    pool.wait_ge(s_x, t * 16 + 16)
                    pool.wait_ge(s_gb_a, t + 1)
                    for a in range(NB):
                        last = nc.gpsimd.tensor_tensor(x_bias[:, a, :], x_in[:, a, :], gb_a[:, :], ALU.add)
                    last.then_inc(s_x_bias, 1)
                if has("stats_x"):
                    deviation(t, "stats_x", 2)
                if has("stats_m"):
                    deviation(t, "stats_m", 2)
                if has("stats_y"):
                    for a in range(NB):
                        last = nc.gpsimd.tensor_tensor(x1_bias[:, a, :], x1[:, a, :], bc_cproj[:, :], ALU.add)
                    last.then_inc(s_x1_bias, 1)

            steps(pool, step)

        @block.tensor
        def _(pe):
            pe.wait_ge(s_ident, 3)
            pe.wait_ge(s_small, 16 * 8)
            pe.wait_ge(s_bias_rows, 1)
            nc.tensor.transpose(scan_bank[0][:, 0:32], bias_rows, ident[0:32, 0:32])
            nc.tensor.transpose(scan_bank[0][:, 32:64], turned_rows, ident[0:32, 0:32])
            pe.wait_ge(s_silu, 1)
            for c in range(CB):
                last = nc.tensor.transpose(scan_bank[1][:, c * B:(c + 1) * B],
                                           cond_sb[:, 2, c * 128:(c + 1) * 128], ident[0:B, 0:B])
            last.then_inc(s_startT, 1)
            pe.wait_ge(s_startC, 1)
            pe.wait_ge(s_wmod, 16)
            wmod = P[:, :, :, :].rearrange("p a b c -> p (a b c)")[:, 0:CB * 6 * H].rearrange("p (c n) -> p c n", c=CB)
            for k, blk in enumerate((0, 1, 2, 3, 6, 7, 8, 9)):
                for c in range(CB):
                    last = nc.tensor.matmul(score_bank[0][:, k * B:(k + 1) * B], wmod[:, c, blk * 128:(blk + 1) * 128],
                                            silu_T[:, c, :], start=(c == 0), stop=(c == CB - 1))
            last.then_inc(s_mod, 1)
            for i in range(2):
                for c in range(CB):
                    last = nc.tensor.matmul(score_bank[1][0:B, i * H:(i + 1) * H], silu_T[:, c, :],
                                            wmod[:, c, (3 * i + 2) * H:(3 * i + 3) * H],
                                            start=(c == 0), stop=(c == CB - 1))
            last.then_inc(s_mod, 1)
            pe.wait_ge(s_modC, 2)

            def take(t, stage, use):
                wait(pe, s_bank_done, before(BANK_USES, t, stage) + use - 1)
                return bank[bank_of(t, stage, use)]

            def transposes(t, stage, use, src):
                to = take(t, stage, use)
                for c in range(CB):
                    for a in range(NB):
                        last = nc.tensor.transpose(to[:, c * N + a * 128:c * N + (a + 1) * 128],
                                                   src[:, a, c * 128:(c + 1) * 128], ident[:, :])
                last.then_inc(s_bank_full, 1)

            def columns(t, stage, use, w, xT, blocks):
                to = take(t, stage, use)
                for i, blk in enumerate(blocks):
                    n = 0
                    for c in range(CB):
                        for a, b in PARTS:
                            last = nc.tensor.matmul(to[:, i * N:(i + 1) * N], w[a][:, c, blk * 128:(blk + 1) * 128],
                                                    xT[:, b, c, :], start=(n == 0), stop=(n == 3 * CB - 1))
                            n += 1
                last.then_inc(s_bank_full, 1)

            def tokens(to, xT, w, c0, blocks, at, a):
                n = 0
                for c in range(blocks):
                    for i, j in PARTS:
                        last = nc.tensor.matmul(to[:, at:at + H], xT[:, i, c, a * 128:(a + 1) * 128],
                                                w[j][:, c, c0:c0 + H], start=(n == 0), stop=(n == 3 * blocks - 1))
                        n += 1
                return last

            def values(t, stage, w, c0, xT):
                to = take(t, stage, 0)
                for a in range(NB):
                    last = tokens(to, xT, w, c0, CB, a * H, a)
                last.then_inc(s_bank_full, 1)

            def maxima(t, stage, half):
                to = take(t, stage, 0)
                pe.wait_ge(s_max, before(MAXIMA, t, stage))
                for a in range(NB):
                    last = nc.tensor.transpose(to[0:NH, a * 128:(a + 1) * 128],
                                               MH[:, half, a, :, :, :].rearrange("p a b c -> p (a b c)").bitcast(fp32),
                                               ident[:, :])
                last.then_inc(s_bank_full, 1)

            def outputs(t, stage, w, attend):
                to = take(t, stage, 0)
                pe.wait_ge(s_OT, before(HALVES, t, attend))
                for a in range(NB):
                    last = tokens(to, OT, w, 0, 2, a * H, a)
                last.then_inc(s_bank_full, 1)

            def up(t):
                pe.wait_ge(s_bank_done, before(BANK_USES, t - 1, "T_m") + 1)
                for u in range(FB // 2):
                    columns(t, "mlp_up", u, w_mlp1, xT_m, (2 * u, 2 * u + 1))

            def down(t, a):
                if a == 0:
                    pe.wait_ge(s_hidden_lo, (t - 3) * 4 + 4)
                to = take(t, f"down{a}", 0)
                tokens(to, HH, w_mlp2, 0, FB, 0, a).then_inc(s_bank_full, 1)

            def transposed(t, stage, ready, count, src):
                pe.wait_ge(ready, count)
                transposes(t, stage, 0, src)

            def split_of(t, stage):
                pe.wait_ge(s_bank_done, before(BANK_USES, t, stage) + 1)

            def q_y(t):
                split_of(t, "T_y")
                columns(t, "q_y", 0, w_qc, xT_y, (0, 1))

            def k_y(t):
                split_of(t, "T_c")
                columns(t, "k_y", 0, w_kvc, xT_c, (0, 1))

            def q_x(t):
                split_of(t, "T_x")
                columns(t, "q_x", 0, w_qkv, xT_x, (0, 1))

            tasks = {
                "mlp_up": up,
                "out_x": lambda t: outputs(t, "out_x", w_proj, "attend_y"),
                "T_y": lambda t: transposed(t, "T_y", s_xn_y, t, xn_a),
                "T_c": lambda t: transposed(t, "T_c", s_xn_c, t, xn_b),
                "q_y": q_y,
                "k_y": k_y,
                "max_x0": lambda t: maxima(t, "max_x0", 0),
                "max_x1": lambda t: maxima(t, "max_x1", 1),
                "down0": lambda t: down(t, 0),
                "T_x": lambda t: transposed(t, "T_x", s_xn_x, t + 2, xn_b),
                "down1": lambda t: down(t, 1),
                "out_y": lambda t: outputs(t, "out_y", w_cproj, "attend_x"),
                "T_m": lambda t: transposed(t, "T_m", s_xn_m, t - 1, xn_a),
                "q_x": q_x,
                "k_x": lambda t: columns(t, "k_x", 0, w_qkv, xT_x, (2, 3)),
                "max_y0": lambda t: maxima(t, "max_y0", 0),
                "max_y1": lambda t: maxima(t, "max_y1", 1),
            }

            def heads(letter, t, has, s1, s2):
                scan, attend = "scan_" + s1, "attend_" + s2
                scans = before(SCANS, t, scan)
                scores = before(ATTENDS, t, attend)

                def weighted(grp):
                    half, g = divmod(grp, 2)
                    pe.wait_ge(s_exp, scores + 4 * grp + 4)
                    if g == 0:
                        wait(pe, s_pv_read, before(HALVES, t, attend) + half - 1)
                    for kb in range(NB):
                        for j in range(4):
                            last = nc.tensor.matmul(
                                pv_bank[half][32 * j:32 * j + 32, g * N:(g + 1) * N],
                                V[s2][:, kb, head_of(half, g, j), :],
                                P[:, (4 * grp + j) % 8, kb, :], start=(kb == 0), stop=(kb == NB - 1))
                    last.then_inc(s_pv, 1)

                def slot(s):
                    p, par = divmod(s, 2)
                    if has(scan):
                        if s % PAIRS == 0:
                            pe.wait_ge(s_load[s1][s // PAIRS], before(LOADS[s1], t, scan) * 16)
                        wait(pe, s_scan_done, scans + s - 1)
                        for a in range(NB):
                            last = nc.tensor.matmul(
                                scan_bank[s % 2][:, a * N:(a + 1) * N],
                                QS[s1][64 * par:64 * par + 3 * HD, p, a * 128:(a + 1) * 128],
                                KS[s1][64 * par:64 * par + 3 * HD, p, :], start=True, stop=True)
                        last.then_inc(s_scan_full, 1)
                    if has(attend):
                        if s % PAIRS == 0:
                            pe.wait_ge(s_row[s // PAIRS], before(ROWS[s // PAIRS], t, attend) * 16)
                        wait(pe, s_exp, scores + s - 1)
                        for kb in range(NB):
                            last = nc.tensor.matmul(
                                score_bank[s % 2][:, kb * N:(kb + 1) * N],
                                KS[s2][64 * par:64 * par + 3 * HD + 2, p, kb * 128:(kb + 1) * 128],
                                QS[s2][64 * par:64 * par + 3 * HD + 2, p, :], start=True, stop=True)
                        last.then_inc(s_score_full, 1)
                        if s >= 5 and (s - 5) % 4 == 0:
                            weighted((s - 5) // 4)

                def last_values(t):
                    if has(attend):
                        weighted(3)
                    if has("v_" + s2):
                        if s2 == "y":
                            values(t, "v_y", w_kvc, H, xT_c)
                        else:
                            values(t, "v_x", w_qkv, 2 * H, xT_x)

                section(letter, t, lambda name: name[:2] == "v_" or has(name), slot, {**tasks, "v_" + s2: last_values})

            def step(t, has):
                if isinstance(t, int) and t == 1:
                    pe.wait_ge(s_weight_lo, 4)
                heads("A", t, has, "x", "y")
                if isinstance(t, int) and t == FIRST:
                    pe.wait_ge(s_weight_lo, 1)
                heads("B", t, has, "y", "x")

            steps(pe, step)

        @block.scalar
        def _(act):
            act.wait_ge(s_small, 16 * 8)
            nc.scalar.activation(cond_sb[:, 1, :], cond_sb[:, 0, :], ACT.Exp, scale=-1.0).then_inc(s_exp0, 1)

            def split_weights(i):
                act.wait_ge(s_weight[i], 16 * (2, 33, 1, 1)[i])
                for dst, src in weight_views(i, HI):
                    last = nc.scalar.activation(dst, src, ACT.Copy)
                last.then_inc(s_weight_hi, 1)

            split_weights(0)

            def full(t, stage, use=0):
                act.wait_ge(s_bank_full, before(BANK_USES, t, stage) + use + 1)
                return bank[bank_of(t, stage, use)]

            def copied(t, stage, dst):
                src = full(t, stage)
                nc.scalar.activation(dst[:, HI, :, :].rearrange("p c n -> p (c n)"), src[:, :],
                                     ACT.Copy).then_inc(s_bank_hi, 1)

            def modulated(t, stage, mod, loaded, count):
                act.wait_ge(loaded, count)
                src = full(t, stage)
                for c in range(CB):
                    last = nc.scalar.activation(xm[:, c, :], src[:, c * N:(c + 1) * N], ACT.Identity,
                                                bias=mod[:, c:c + 1], scale=mod[:, 2 + c:3 + c])
                last.then_inc(s_bank_hi, 1)

            def projected(t, stage, dst, col):
                if stage[0] == "q":
                    for s in "xy":
                        for half in range(2):
                            wait(act, s_load[s][half], before(LOADS[s], t, stage) * 16)
                src = full(t, stage)
                for i in range(2):
                    last = nc.scalar.activation(dst[:, HI, i, :], src[:, i * N:(i + 1) * N], ACT.Identity,
                                                bias=bias_cols[:, col + i:col + i + 1])
                last.then_inc(s_bank_hi, 1)

            def up(t):
                for u in range(FB // 2):
                    src = full(t, "mlp_up", u)
                    wait(act, s_hidden_lo, (t - 3) * 4 + u - 1)
                    for i in range(2):
                        col = MLPC + 2 * u + i
                        last = nc.scalar.activation(HF[:, u % 2, i, :], src[:, i * N:(i + 1) * N],
                                                    ACT.Gelu_apprx_tanh, bias=bias_cols[:, col:col + 1])
                    last.then_inc(s_bank_hi, 1)

            tasks = {
                "mlp_up": up,
                "T_y": lambda t: copied(t, "T_y", xT_y),
                "T_c": lambda t: copied(t, "T_c", xT_c),
                "q_y": lambda t: projected(t, "q_y", SQ, 32 + QCC),
                "k_y": lambda t: projected(t, "k_y", SK, 32 + KVCC),
                "T_x": lambda t: modulated(t, "T_x", mod_x, s_modx, (t + 1) * 16 + 16),
                "T_m": lambda t: modulated(t, "T_m", mod_m, s_modm, (t - 2) * 16 + 16),
                "q_x": lambda t: projected(t, "q_x", SQ, 32 + QKVC),
                "k_x": lambda t: projected(t, "k_x", SK, 32 + QKVC + 2),
            }

            def heads(letter, t, has, attend):
                scores = before(ATTENDS, t, attend)

                def slot(s):
                    if has(attend):
                        act.wait_ge(s_score_full, scores + s + 1)
                        if s % 4 == 0:
                            wait(act, s_pv, before(GROUPS, t, attend) + s // 4 - 1)
                        nc.scalar.activation(P[:, s % 8, :, :].rearrange("p a n -> p (a n)"), score_bank[s % 2][:, :],
                                             ACT.Exp, scale=SCALE).then_inc(s_exp, 1)

                section(letter, t, has, slot, tasks)

            def step(t, has):
                if isinstance(t, int) and t == 0:
                    split_weights(1)
                heads("A", t, has, "attend_y")
                if isinstance(t, int) and t == 0:
                    split_weights(2)
                    split_weights(3)
                    act.wait_ge(s_weight_lo, 4)
                heads("B", t, has, "attend_x")

            steps(act, step)

        @block.vector
        def _(dve):
            nc.vector.memset(QS["x"][:, :, :].bitcast(fp32), 0.0)
            nc.vector.memset(QS["y"][:, :, :].bitcast(fp32), 0.0)
            dve.wait_ge(s_small, 16 * 8)
            nc.vector.tensor_copy(turned_rows.rearrange("p (b d h) -> p b h d", d=HD, h=PAIRS // 2),
                                  bias_rows.rearrange("p (b h d) -> p b h d", d=HD, h=PAIRS // 2))\
                .then_inc(s_bias_rows, 1)
            dve.wait_ge(s_exp0, 1)
            nc.vector.tensor_scalar_add(cond_sb[:, 2, :], cond_sb[:, 1, :], 1.0).then_inc(s_silu_part, 1)
            dve.wait_ge(s_silu_part, 1)
            nc.vector.reciprocal(cond_sb[:, 1, :], cond_sb[:, 2, :]).then_inc(s_silu_part, 1)
            dve.wait_ge(s_silu_part, 2)
            nc.vector.tensor_tensor(cond_sb[:, 2, :], cond_sb[:, 1, :], cond_sb[:, 0, :], ALU.mult).then_inc(s_silu, 1)
            dve.wait_ge(s_startT, 1)
            nc.vector.tensor_copy(bias_cols[:, :], scan_bank[0][:, 0:64])
            nc.vector.tensor_copy(silu_T[:, :, :].rearrange("p c b -> p (c b)"),
                                  scan_bank[1][:, 0:CB * B]).then_inc(s_startC, 1)
            dve.wait_ge(s_startC, 1)
            dve.wait_ge(s_mod, 1)
            for k, blk in enumerate((0, 1, 2, 3, 6, 7, 8, 9)):
                last = nc.vector.tensor_scalar(mod_all[:, :, k], score_bank[0][:, k * B:(k + 1) * B],
                                               bias_cols[:, blk:blk + 1], float(k % 4 // 2), ALU.add, ALU.add)
            last.then_inc(s_modC, 1)
            dve.wait_ge(s_mod, 2)
            dve.wait_ge(s_small, 16 * 8)
            nc.vector.tensor_tensor(gate_all, score_bank[1][0:B, :], gate_bias, ALU.add).then_inc(s_modC, 1)

            def split_weights(i):
                dve.wait_ge(s_weight_hi, i + 1)
                for (dst, src), (high, _) in zip(weight_views(i, LO), weight_views(i, HI)):
                    last = nc.vector.tensor_tensor(dst, src, high.bitcast(fp32), ALU.subtract)
                last.then_inc(s_weight_lo, 1)

            split_weights(0)
            dve.wait_ge(s_const, 16 * 5)
            dve.wait_ge(s_ident, 3)

            def link(t, stage, instruction):
                instruction.then_inc(s_link, 1)
                dve.wait_ge(s_link, before(LINKS, t, stage) + 1)

            def full(t, stage, use=0):
                dve.wait_ge(s_bank_full, before(BANK_USES, t, stage) + use + 1)
                return bank[bank_of(t, stage, use)]

            def hi_done(t, stage, use=0):
                dve.wait_ge(s_bank_hi, before(ACT_USES, t, stage) + use + 1)

            def stats_of(t, stage, inputs):
                k = 0
                for src in inputs:
                    for a in range(NB):
                        last = nc.vector.bn_stats(stats[:, k, :], src[:, a, :])
                        k += 1
                link(t, stage, last)
                nc.vector.memset(spare[:, :], 0.0)
                for i in range(k):
                    last = nc.vector.bn_aggr(mv[:, i, :], stats[:, i, :])
                last.then_inc(s_mv, 1)

            def apply(t, stage, pairs):
                dve.wait_ge(s_mv, before(NORMS, t, stage))
                dve.wait_ge(s_rstd, before(NORMS, t, stage))
                k = 0
                for src, dst, ready in pairs:
                    for a in range(NB):
                        last = nc.vector.tensor_scalar(dst[:, a, :], src[:, a, :], mv[:, k, 0:1], rstd[:, k:k + 1],
                                                       ALU.subtract, ALU.mult)
                        k += 1
                    last.then_inc(ready, 1)

            def split_modulated(t, stage, xT):
                hi_done(t, stage)
                link(t, stage, nc.vector.tensor_copy(xT[:, HI, :, :], xm[:, :, :]))
                nc.vector.tensor_tensor(xT[:, LO, :, :], xm[:, :, :], xT[:, HI, :, :].bitcast(fp32),
                                        ALU.subtract).then_inc(s_bank_done, 1)

            def split_copied(t, stage, xT):
                src = full(t, stage)
                hi_done(t, stage)
                nc.vector.tensor_tensor(xT[:, LO, :, :].rearrange("p c n -> p (c n)"), src[:, :],
                                        xT[:, HI, :, :].rearrange("p c n -> p (c n)").bitcast(fp32),
                                        ALU.subtract).then_inc(s_bank_done, 1)

            def projected(t, stage, dst, col):
                src = full(t, stage)
                hi_done(t, stage)
                for i in range(2):
                    last = nc.vector.scalar_tensor_tensor(
                        out=dst[:, LO, i, :], in0=src[:, i * N:(i + 1) * N], scalar=bias_cols[:, col + i:col + i + 1],
                        in1=dst[:, HI, i, :].bitcast(fp32), op0=ALU.add, op1=ALU.subtract)
                last.then_inc(s_bank_done, 1)

            def values(t, s):
                src = full(t, "v_" + s)
                for a in range(NB):
                    last = nc.vector.tensor_tensor(
                        V[s][:, a, :, 0:HD], src[:, a * H:(a + 1) * H].rearrange("p (h d) -> p h d", d=HD),
                        bc_v[s][:, :].rearrange("p (h d) -> p h d", d=HD), ALU.add)
                last.then_inc(s_bank_done, 1)

            def normalise(t, stage, half):
                done = before(HALVES, t, stage) + half

                def link_pv(n, instruction):
                    instruction.then_inc(s_link_pv, 1)
                    dve.wait_ge(s_link_pv, done * 4 + n)

                dve.wait_ge(s_pv, before(GROUPS, t, stage) + 2 * half + 2)
                nc.vector.transpose(PT[:, :, :, :].rearrange("p a b c -> p (a b c)"), pv_bank[half][:, :])\
                    .then_inc(s_pv_read, 1)
                dve.wait_ge(s_pv_read, done + 1)
                link_pv(1, nc.vector.reciprocal(rsum[:, :, :], PT[:, :, :, HD]))
                link_pv(2, nc.vector.tensor_tensor(PN[:, :, :, :].rearrange("p b a d -> p a b d"), PT[:, :, :, 0:HD],
                                                   rsum[:, :, :].unsqueeze(3).to_broadcast([128, 2, 8, HD]), ALU.mult))
                link_pv(3, nc.vector.transpose(PO[:, :], PN[:, :, :, :].rearrange("p a b c -> p (a b c)")))
                link_pv(4, nc.vector.tensor_copy(OT[:, HI, half, :], PO[:, :]))
                nc.vector.tensor_tensor(OT[:, LO, half, :], PO[:, :], OT[:, HI, half, :].bitcast(fp32),
                                        ALU.subtract).then_inc(s_OT, 1)

            def split_maxima(t, s, half):
                dve.wait_ge(s_scan_done, before(SCANS, t, "scan_" + s) + PAIRS * (half + 1))
                src = MX[:, :, half, :, :]
                link(t, f"split_{s}{half}", nc.vector.tensor_copy(MH[:, half, :, :, HI, :], src))
                nc.vector.tensor_tensor(MH[:, half, :, :, LO, :], src, MH[:, half, :, :, HI, :].bitcast(fp32),
                                        ALU.subtract).then_inc(s_max, 1)

            def copy_maxima(t, s, half):
                stage = f"max_{s}{half}"
                src = full(t, stage)
                wait(dve, s_row[half], before(ROWS[half], t, stage) * 16)
                nc.vector.tensor_copy(MT[half][:, :], src[0:NH, 0:N]).then_inc(s_bank_done, 1)

            def out_x(t):
                src = full(t, "out_x")
                for a in range(NB):
                    last = nc.vector.tensor_tensor(gated[:, a, :], src[:, a * H:(a + 1) * H], gate_a[:, :], ALU.mult)
                last.then_inc(s_bank_done, 1)
                dve.wait_ge(s_bank_done, before(BANK_USES, t, "out_x") + 1)
                dve.wait_ge(s_x_bias, t)
                wait(dve, s_x1_bias, t - 1)
                nc.vector.tensor_tensor(x1[:, :, :], gated[:, :, :], x_bias[:, :, :], ALU.add).then_inc(s_x1, 1)

            def out_y(t):
                src = full(t, "out_y")
                dve.wait_ge(s_x1_bias, t - 1)
                wait(dve, s_x2_bias, t - 2)
                nc.vector.tensor_tensor(x2[:, :, :].rearrange("p a c -> p (a c)"), src[:, :],
                                        x1_bias[:, :, :].rearrange("p a c -> p (a c)"),
                                        ALU.add).then_inc(s_bank_done, 1)

            def up(t):
                for u in range(FB // 2):
                    hi_done(t, "mlp_up", u)
                    nc.vector.tensor_copy(HH[:, HI, 2 * u:2 * u + 2, :], HF[:, u % 2, :, :]).then_inc(s_bank_done, 1)

            def down(t, a):
                if a == 0:
                    dve.wait_ge(s_x2_bias, t - 2)
                    wait(dve, s_out, (t - 3) * 16)
                src = full(t, f"down{a}")
                nc.vector.tensor_tensor(y[:, a, :], src[:, 0:H], gate_m[:, :], ALU.mult).then_inc(s_bank_done, 1)
                dve.wait_ge(s_bank_done, before(BANK_USES, t, f"down{a}") + 1)
                nc.vector.tensor_tensor(y[:, a, :], y[:, a, :], x2_bias[:, a, :], ALU.add).then_inc(s_y, 1)

            def stats_y(t):
                dve.wait_ge(s_c, t * 16)
                dve.wait_ge(s_x1, t)
                stats_of(t, "stats_y", (x1, c_in))

            def stats_x(t):
                dve.wait_ge(s_x, (t + 1) * 16 + 16)
                stats_of(t, "stats_x", (x_in,))

            def stats_m(t):
                dve.wait_ge(s_bank_done, before(BANK_USES, t, "out_y") + 1)
                stats_of(t, "stats_m", (x2,))

            tasks = {
                "mlp_up": up,
                "out_x": out_x,
                "stats_y": stats_y,
                "apply_y": lambda t: apply(t, "apply_y", ((x1, xn_a, s_xn_y), (c_in, xn_b, s_xn_c))),
                "T_y": lambda t: split_copied(t, "T_y", xT_y),
                "T_c": lambda t: split_copied(t, "T_c", xT_c),
                "q_y": lambda t: projected(t, "q_y", SQ, 32 + QCC),
                "k_y": lambda t: projected(t, "k_y", SK, 32 + KVCC),
                "split_x0": lambda t: split_maxima(t, "x", 0),
                "max_x0": lambda t: copy_maxima(t, "x", 0),
                "v_y": lambda t: values(t, "y"),
                "split_x1": lambda t: split_maxima(t, "x", 1),
                "max_x1": lambda t: copy_maxima(t, "x", 1),
                "stats_x": stats_x,
                "apply_x": lambda t: apply(t, "apply_x", ((x_in, xn_b, s_xn_x),)),
                "down0": lambda t: down(t, 0),
                "T_x": lambda t: split_modulated(t, "T_x", xT_x),
                "down1": lambda t: down(t, 1),
                "out_y": out_y,
                "stats_m": stats_m,
                "apply_m": lambda t: apply(t, "apply_m", ((x2, xn_a, s_xn_m),)),
                "T_m": lambda t: split_modulated(t, "T_m", xT_m),
                "q_x": lambda t: projected(t, "q_x", SQ, 32 + QKVC),
                "k_x": lambda t: projected(t, "k_x", SK, 32 + QKVC + 2),
                "split_y0": lambda t: split_maxima(t, "y", 0),
                "max_y0": lambda t: copy_maxima(t, "y", 0),
                "v_x": lambda t: values(t, "x"),
                "split_y1": lambda t: split_maxima(t, "y", 1),
                "max_y1": lambda t: copy_maxima(t, "y", 1),
            }

            def heads(letter, t, has, scan, attend):
                def slot(s):
                    if has(scan):
                        p, par = divmod(s, 2)
                        half, p = divmod(p, PAIRS // 2)
                        dve.wait_ge(s_scan_full, before(SCANS, t, scan) + s + 1)
                        nc.vector.tensor_reduce(MX[:, :, half, par, p], scan_bank[s % 2][:, :].rearrange("p (a n) -> p a n", a=NB),
                                                AXIS.X, ALU.max, negate=True).then_inc(s_scan_done, 1)
                    if has(attend) and s == 12:
                        normalise(t, attend, 0)

                section(letter, t, has, slot, tasks)
                if has(attend):
                    normalise(t, attend, 1)

            def step(t, has):
                if isinstance(t, int) and t == 0:
                    split_weights(1)
                heads("A", t, has, "scan_x", "attend_y")
                if isinstance(t, int) and t == 0:
                    split_weights(2)
                    split_weights(3)
                heads("B", t, has, "scan_y", "attend_x")

            steps(dve, step)


_INS = ["x", "cond_1024", "ctx_1024"] + ["L0_xcond_" + n for n in (
    "W_mod", "b_mod", "W_qkv", "b_qkv", "W_proj", "b_proj", "W_qc", "b_qc", "W_kvc", "b_kvc",
    "W_cproj", "b_cproj", "W_mlp1", "b_mlp1", "W_mlp2", "b_mlp2")]


def kernel(**inputs):
    import numpy as np
    import concourse.bacc as bacc
    from concourse.bass_utils import run_bass_kernel_spmd

    nc = bacc.Bacc("TRN2", target_bir_lowering=False, num_devices=1)
    arrays, args = {}, []
    for name in _INS:
        a = np.ascontiguousarray(inputs[name])
        arrays["in_" + name] = a
        args.append(nc.dram_tensor("in_" + name, a.shape, mybir.dt.from_np(a.dtype), kind="ExternalInput").ap())
    args.append(nc.dram_tensor("out_x", (B, N, H), fp32, kind="ExternalOutput").ap())
    build(nc, *args)
    r = run_bass_kernel_spmd(nc, [arrays], core_ids=[0])
    return r.results[0]["out_x"]
```

```python
import concourse.bass as bass
from concourse import mybir
from contextlib import ExitStack

fp32 = mybir.dt.float32
f32r = mybir.dt.float32r
ALU = mybir.AluOpType
ACT = mybir.ActivationFunctionType
AXIS = mybir.AxisListType

B, N, H, NH, MLP = 16, 256, 256, 16, 1024
HD = H // NH
CB = H // 128
NB = N // 128
FB = MLP // 128
PAIRS = NH // 2
EPS = 1e-6
SCALE = HD ** -0.5
HI, LO = 0, 1

PLAN = {
    "A": [("scan_x", 0, 0, 0), ("attend_y", -2, 0, 0),
          ("split_y1", -2, 0, 0),
          ("stats_c", -1, 0, 0),
          ("up0", -3, 0, 1), ("up1", -3, 0, 1),
          ("pv_x3", -1, 1, 1),
          ("max_y1", -2, 2, 2),
          ("norm_x1", -1, 2, 2),
          ("apply_c", -1, 3, 3),
          ("out_x", -1, 4, 4),
          ("stats_y", -1, 4, 4),
          ("T_c", -1, 5, 5),
          ("pv_y0", -2, 5, 6), ("apply_y", -1, 6, 6), ("T_y", -1, 7, 8),
          ("split_x0", 0, 8, 8),
          ("k_y", -1, 8, 9), ("q_y", -1, 9, 10), ("pv_y1", -2, 9, 10),
          ("max_x0", 0, 10, 11),
          ("up2", -3, 11, 12), ("up3", -3, 11, 12),
          ("norm_y0", -2, 13, 13), ("pv_y2", -2, 13, 13), ("v_x", 0, 14, 15)],
    "B": [("scan_y", -1, 0, 0), ("attend_x", 0, 0, 0),
          ("split_x1", 0, 0, 0),
          ("stats_x", 1, 0, 0),
          ("down0", -3, 0, 1),
          ("pv_y3", -2, 1, 1),
          ("max_x1", 0, 2, 2),
          ("norm_y1", -2, 2, 2), ("apply_x", 1, 3, 3),
          ("out_y", -2, 4, 5),
          ("T_x", 1, 5, 6),
          ("stats_m", -2, 6, 6), ("pv_x0", 0, 6, 6),
          ("k_x", 1, 8, 8), ("apply_m", -2, 8, 8), ("split_y0", -1, 8, 8),
          ("q_x", 1, 9, 9), ("T_m", -2, 9, 10),
          ("pv_x1", 0, 9, 9), ("max_y0", -1, 10, 11),
          ("v_y", -1, 11, 12),
          ("norm_x0", 0, 12, 13), ("pv_x2", 0, 13, 13), ("down1", -3, 14, 15)],
}
STAGES = [(name, shift) for section in "AB" for name, shift, _, _ in PLAN[section]]
RANK = {name: i for i, (name, _) in enumerate(STAGES)}
SHIFT = dict(STAGES)
FIRST, LAST = -1, B + 2
LOOP = (4, B - 1)

UPS = [f"up{u}" for u in range(FB // 2)]
ACT_USES = {n: 1 for n in ("T_y", "T_c", "q_y", "k_y", "T_x", "T_m", "q_x", "k_x", *UPS)}
BANK_USES = ACT_USES | {n: 1 for n in ("out_x", "max_x0", "max_x1", "v_x", "out_y", "max_y0", "max_y1", "v_y",
                                       "down0", "down1")}
SCANS = {"scan_x": NH, "scan_y": NH}
ATTENDS = {"attend_x": NH, "attend_y": NH}
GROUPS = {f"pv_{s}{g}": 1 for s in "xy" for g in range(4)}
HALVES = {f"norm_{s}{h}": 1 for s in "xy" for h in range(2)}
NORMS = {"stats_c": 1, "stats_y": 1, "stats_m": 1, "stats_x": 1}
LOADS = {"x": {"q_x": 12}, "y": {"q_y": 12}}
MAXIMA = {"split_x0": 1, "split_x1": 1, "split_y0": 1, "split_y1": 1}
ROWS = [{"max_x0": 2, "max_y0": 2}, {"max_x1": 2, "max_y1": 2}]
LINKS = {n: 1 for n in ("stats_c", "stats_y", "stats_x", "stats_m", "T_x", "T_m", *MAXIMA)}


def build(nc, x, cond, ctx_in, W_mod, b_mod, W_qkv, b_qkv, W_proj, b_proj, W_qc, b_qc, W_kvc, b_kvc,
          W_cproj, b_cproj, W_mlp1, b_mlp1, W_mlp2, b_mlp2, out):
    def before(per, t, stage):
        def at(step, clamp):
            total = 0
            for name, n in per.items():
                ran = step + SHIFT[name] + (1 if RANK[name] < RANK[stage] else 0)
                total += n * (min(max(ran, 0), B) if clamp else ran)
            return total
        if isinstance(t, int):
            return at(t, True)
        slope = at(1, False) - at(0, False)
        base = at(0, False)
        return t * slope + base if slope else base

    def bank_of(t, stage, use):
        return (before(BANK_USES, t if isinstance(t, int) else LOOP[0], stage) + use) % 2

    def wait(eng, sem, value):
        if not isinstance(value, int) or value > 0:
            eng.wait_ge(sem, value)

    def head_of(half, g, j):
        return (2 * (2 * half + g) + j // 2) + PAIRS * (j % 2)

    es = ExitStack()
    with es:
        def sb(name, shape, dt=fp32):
            return es.enter_context(nc.sbuf_tensor(name, shape, dt))

        def sem(name):
            return es.enter_context(nc.semaphore(name))

        def dram(name, shape, dt=fp32):
            return nc.dram_tensor(name, shape, dt, kind="Internal").ap()

        WT = sb("WT", [128, 2, 4 * 2048], f32r)

        def weight(start, blocks, cols):
            return [WT[:, part, start:start + blocks * cols].rearrange("p (c n) -> p c n", c=blocks)
                    for part in (HI, LO)]

        w_qkv = weight(0, CB, 3 * H)
        w_qc = weight(1536, CB, H)
        w_kvc = weight(2048, CB, 2 * H)
        w_proj = weight(3072, 2, H)
        w_cproj = weight(3584, 2, H)
        w_mlp1 = weight(4096, CB, MLP)
        w_mlp2 = weight(6144, FB, H)

        QS = {s: sb(f"QS_{s}", [128, PAIRS, N], f32r) for s in "xy"}
        KS = {s: sb(f"KS_{s}", [128, PAIRS, N], f32r) for s in "xy"}
        V = {s: sb(f"V_{s}", [128, NB, NH, 32]) for s in "xy"}
        P = sb("P", [128, 8, NB, N])
        SQ = sb("SQ", [128, 2, 2, N], f32r)
        SK = sb("SK", [128, 2, 2, N], f32r)
        xT_x = sb("xT_x", [128, 2, CB, N], f32r)
        xT_y = sb("xT_y", [128, 2, CB, N], f32r)
        xT_c = sb("xT_c", [128, 2, CB, N], f32r)
        xT_m = sb("xT_m", [128, 2, CB, N], f32r)
        HH = sb("HH", [128, 2, FB, N], f32r)
        HF = sb("HF", [128, 2, 2, N])
        xn_a = sb("xn_a", [128, NB, H])
        xn_b = sb("xn_b", [128, NB, H])
        x_in = sb("x_in", [128, NB, H])
        c_in = sb("c_in", [128, NB, H])
        x1 = sb("x1", [128, NB, H])
        x1_bias = sb("x1_bias", [128, NB, H])
        x2 = sb("x2", [128, NB, H])
        x2_bias = sb("x2_bias", [128, NB, H])
        x_bias = sb("x_bias", [128, NB, H])
        y = sb("y", [128, NB, H])
        xm = sb("xm", [128, CB, N])
        gated = xm
        PT = sb("PT", [128, 2, 8, 32])
        PN = sb("PN", [128, 8, 2, HD])
        PO = sb("PO", [128, N])
        OT = sb("OT", [128, 2, 2, N], f32r)
        rsum = sb("rsum", [128, 2, 8])
        MX = sb("MX", [128, NB, 2, 2, PAIRS // 2])
        MH = sb("MH", [128, 2, NB, 2, 2, PAIRS // 2], f32r)
        MT = [sb(f"MT{i}", [NH, N], f32r) for i in range(2)]
        stats = sb("stats", [128, 4, 6])
        mv = sb("mv", [128, 4, 2])
        rstd = sb("rstd", [128, 4])
        var_eps = sb("var_eps", [128, 4])
        minus_half = sb("minus_half", [128, 4])
        eps = sb("eps", [128, 4])
        spare = sb("spare", [128, 1])
        ident = sb("ident", [128, 128])
        bias_cols = sb("bias_cols", [128, 64])
        bc_v = {"x": sb("bc_v_x", [128, H]), "y": sb("bc_v_y", [128, H])}
        bc_proj = sb("bc_proj", [128, H])
        bc_cproj = sb("bc_cproj", [128, H])
        bc_mlp2 = sb("bc_mlp2", [128, H])
        gb_a = sb("gb_a", [128, H])
        gb_m = sb("gb_m", [128, H])
        gate_a = sb("gate_a", [128, H])
        gate_m = sb("gate_m", [128, H])
        mod_x = sb("mod_x", [128, 4])
        mod_m = sb("mod_m", [128, 4])
        bias_rows = xn_a[0:32, 0, 0:128]
        turned_rows = xn_a[0:32, 1, 0:128]
        cond_sb = HF[0:B, :, :, :].rearrange("p a b c -> p (a b) c")
        silu_T = sb("silu_T", [128, CB, B])
        mod_all = sb("mod_all", [128, B, 8])
        gate_bias = x2_bias[0:B, :, :].rearrange("p a c -> p (a c)")
        gate_all = x2[0:B, :, :].rearrange("p a c -> p (a c)")

        d_mod = dram("d_mod", (B, 128, 8))
        d_gate = dram("d_gate", (B, 2 * H))
        scan_bank = [es.enter_context(nc.psum_tensor(f"scan{i}", [128, 512], fp32)) for i in range(2)]
        score_bank = [es.enter_context(nc.psum_tensor(f"score{i}", [128, 512], fp32)) for i in range(2)]
        pv_bank = [es.enter_context(nc.psum_tensor(f"pv{i}", [128, 512], fp32)) for i in range(2)]
        bank = [es.enter_context(nc.psum_tensor(f"bank{i}", [128, 512], fp32)) for i in range(2)]

        s_ident = sem("s_ident")
        s_const = sem("s_const")
        s_small = sem("s_small")
        s_wmod = sem("s_wmod")
        s_weight = [sem(f"s_weight{i}") for i in range(4)]
        s_weight_hi = sem("s_weight_hi")
        s_weight_lo = sem("s_weight_lo")
        s_silu = sem("s_silu")
        s_silu_part = sem("s_silu_part")
        s_bias_rows = sem("s_bias_rows")
        s_exp0 = sem("s_exp0")
        s_startT = sem("s_startT")
        s_startC = sem("s_startC")
        s_mod = sem("s_mod")
        s_modC = sem("s_modC")
        s_modD = sem("s_modD")
        s_x = sem("s_x")
        s_modx = sem("s_modx")
        s_c = sem("s_c")
        s_gate_a = sem("s_gate_a")
        s_gate_m = sem("s_gate_m")
        s_modm = sem("s_modm")
        s_bank_full = sem("s_bank_full")
        s_bank_hi = sem("s_bank_hi")
        s_bank_done = sem("s_bank_done")
        s_scan_full = sem("s_scan_full")
        s_scan_done = sem("s_scan_done")
        s_score_full = sem("s_score_full")
        s_exp = sem("s_exp")
        s_pv = sem("s_pv")
        s_pv_read = sem("s_pv_read")
        s_OT = sem("s_OT")
        s_max = sem("s_max")
        s_row = [sem(f"s_row{i}") for i in range(2)]
        s_load = {s: [sem(f"s_load_{s}{i}") for i in range(2)] for s in "xy"}
        s_mv = sem("s_mv")
        s_eps = sem("s_eps")
        s_rstd = sem("s_rstd")
        s_xn_y, s_xn_c, s_xn_m, s_xn_x = sem("s_xn_y"), sem("s_xn_c"), sem("s_xn_m"), sem("s_xn_x")
        s_gb_a, s_gb_m = sem("s_gb_a"), sem("s_gb_m")
        s_x_bias = sem("s_x_bias")
        s_x1 = sem("s_x1")
        s_x1_bias = sem("s_x1_bias")
        s_x2_bias = sem("s_x2_bias")
        s_hidden_lo = sem("s_hidden_lo")
        s_y = sem("s_y")
        s_out = sem("s_out")
        s_link = sem("s_link")
        s_link_pv = sem("s_link_pv")
        s_pool = sem("s_pool")

        def weight_views(i, part):
            src = P[:, :, :, :].rearrange("p a b c -> p (a b c)")[:, (i % 2) * 2048:(i % 2 + 1) * 2048]
            dst = WT[:, part, i * 2048:(i + 1) * 2048]

            def turned(lo, hi):
                return (dst[:, lo:hi].rearrange("p (b d h) -> p b h d", d=HD, h=PAIRS // 2),
                        src[:, lo:hi].rearrange("p (b h d) -> p b h d", d=HD, h=PAIRS // 2))

            def plain(lo, hi):
                return dst[:, lo:hi], src[:, lo:hi]

            if i == 0:
                return [turned(0, 2 * H), plain(2 * H, 3 * H), turned(3 * H, 5 * H), plain(5 * H, 6 * H),
                        turned(6 * H, 8 * H)]
            if i == 1:
                return [turned(0, H), plain(H, 2 * H), turned(2 * H, 3 * H), plain(3 * H, 8 * H)]
            return [plain(0, 2048)]

        block = es.enter_context(nc.Block())

        def edge_step(step, t):
            step(t, lambda name: 0 <= t + SHIFT[name] < B)

        def steps(eng, step):
            for t in range(FIRST, LOOP[0]):
                edge_step(step, t)
            with eng.Fori(LOOP[0], LOOP[1]) as t:
                step(t, lambda name: True)
            for t in range(LOOP[1], LAST + 1):
                edge_step(step, t)

        def section(letter, t, has, slot, tasks, column=2):
            for s in range(NH):
                slot(s)
                for stage in PLAN[letter]:
                    name = stage[0]
                    if stage[column] == s and name in tasks and has(name):
                        tasks[name](t)

        MODC, QKVC, QCC, KVCC, MLPC = 0, 12, 18, 20, 24
        PARTS = ((HI, HI), (HI, LO), (LO, HI))

        @block.sync
        def _(sp):
            sp.dma_start(cond_sb[:, 0, :], cond).then_inc(s_small, 16)
            for start, src in ((MODC, b_mod), (QKVC, b_qkv), (QCC, b_qc), (KVCC, b_kvc), (MLPC, b_mlp1)):
                rows = src.rearrange("(k p) -> k p", p=128)
                sp.dma_start(bias_rows[start:start + rows.shape[0], :], rows).then_inc(s_small, 16)
            for i in range(2):
                sp.dma_start(gate_bias[:, i * H:(i + 1) * H],
                             b_mod[(3 * i + 2) * H:(3 * i + 3) * H].partition_broadcast(B)).then_inc(s_small, 16)
            stage_w = P[:, :, :, :].rearrange("p a b c -> p (a b c)")
            sp.dma_start(stage_w[:, 0:CB * 6 * H].rearrange("p (c n) -> p c n", c=CB),
                         W_mod.rearrange("(c p) n -> p c n", p=128)).then_inc(s_wmod, 16)
            for dst, src in ((bc_v["x"], b_qkv[2 * H:3 * H]), (bc_v["y"], b_kvc[H:2 * H]), (bc_proj, b_proj),
                             (bc_cproj, b_cproj), (bc_mlp2, b_mlp2)):
                sp.dma_start(dst[:, :], src.partition_broadcast(128)).then_inc(s_const, 16)

            def load_weights(i):
                if i < 2:
                    sp.wait_ge(s_mod, 2)
                else:
                    sp.wait_ge(s_weight_lo, i - 1)
                to = stage_w[:, (i % 2) * 2048:(i % 2 + 1) * 2048]
                if i == 0:
                    sp.dma_start(to[:, 0:1536].rearrange("p (c n) -> p c n", c=CB),
                                 W_qkv.rearrange("(c p) n -> p c n", p=128)).then_inc(s_weight[i], 16)
                    sp.dma_start(to[:, 1536:2048].rearrange("p (c n) -> p c n", c=CB),
                                 W_qc.rearrange("(c p) n -> p c n", p=128)).then_inc(s_weight[i], 16)
                elif i == 1:
                    sp.dma_start(to[:, 0:1024].rearrange("p (c n) -> p c n", c=CB),
                                 W_kvc.rearrange("(c p) n -> p c n", p=128)).then_inc(s_weight[i], 16)
                    for k, w in enumerate((W_proj, W_cproj)):
                        dst = to[:, 1024 + 512 * k:1536 + 512 * k].rearrange("p (c n) -> p c n", c=2)
                        for g in range(2):
                            for j in range(4):
                                row = 32 * j + HD * g
                                for half in range(2):
                                    head = head_of(half, g, j)
                                    sp.dma_start(dst[row:row + HD, half, :],
                                                 w[head * HD:(head + 1) * HD, :]).then_inc(s_weight[i], 16)
                elif i == 2:
                    sp.dma_start(to.rearrange("p (c n) -> p c n", c=CB),
                                 W_mlp1.rearrange("(c p) n -> p c n", p=128)).then_inc(s_weight[i], 16)
                else:
                    sp.dma_start(to.rearrange("p (c n) -> p c n", c=FB),
                                 W_mlp2.rearrange("(c p) n -> p c n", p=128)).then_inc(s_weight[i], 16)

            sp.wait_ge(s_modC, 1)
            sp.dma_start(d_mod.rearrange("b p k -> p b k"), mod_all[:, :, :]).then_inc(s_modD, 16)
            load_weights(0)
            sp.wait_ge(s_modC, 2)
            sp.dma_start(d_gate, gate_all).then_inc(s_modD, 16)
            sp.wait_ge(s_modD, 32)

            def stack(t, s, which, half):
                src, dst, parts = {"q": (SQ, QS[s], (HI, HI, LO)), "k": (SK, KS[s], (HI, LO, HI))}[which]
                if half == 0:
                    sp.wait_ge(s_bank_done, before(BANK_USES, t, f"{which}_{s}") + 1)
                for par in range(2):
                    for c, part in enumerate(parts):
                        row = 64 * par + HD * c
                        sp.dma_start(dst[row:row + HD, 4 * half:4 * half + 4, :].bitcast(fp32),
                                     src[64 * half:64 * half + 64, part, par, :].bitcast(fp32))\
                            .then_inc(s_load[s][half], 16)

            def second_halves(t, s, attend, has):
                wait(sp, s_score_full, before(ATTENDS, t, attend) + (NH if has(attend) else 0))
                stack(t, s, "k", 1)
                stack(t, s, "q", 1)

            def rows(t, s, half):
                sp.wait_ge(s_bank_done, before(BANK_USES, t, f"max_{s}{half}") + 1)
                for par in range(2):
                    row = 64 * par + 3 * HD
                    sp.dma_start(QS[s][row:row + 2, 4 * half:4 * half + 4, :].bitcast(fp32),
                                 MT[half][8 * par:8 * par + 8, :].bitcast(fp32)).then_inc(s_row[half], 16)

            def step(t, has):
                if has("down0"):
                    wait(sp, s_y, (t - 3) * 2)
                    sp.dma_start(gate_m[:, :], d_gate[t - 3, H:2 * H].partition_broadcast(128)).then_inc(s_gate_m, 16)
                if has("max_y1"):
                    rows(t, "y", 1)
                if has("T_m"):
                    sp.dma_start(mod_m[:, :], d_mod[t - 2, :, 4:8]).then_inc(s_modm, 16)
                if has("scan_x"):
                    wait(sp, s_x1, t)
                    sp.dma_start(gate_a[:, :], d_gate[t, 0:H].partition_broadcast(128)).then_inc(s_gate_a, 16)
                if has("scan_x"):
                    wait(sp, s_xn_c, t)
                    sp.dma_start(c_in[:, :, :], ctx_in[t].rearrange("(a p) c -> p a c", p=128)).then_inc(s_c, 16)
                if has("k_y"):
                    stack(t, "y", "k", 0)
                if has("q_y"):
                    stack(t, "y", "q", 0)
                if has("max_x0"):
                    rows(t, "x", 0)
                if has("stats_x"):
                    wait(sp, s_x_bias, t + 1)
                    sp.dma_start(x_in[:, :, :], x[t + 1].rearrange("(a p) c -> p a c", p=128)).then_inc(s_x, 16)
                    sp.dma_start(mod_x[:, :], d_mod[t + 1, :, 0:4]).then_inc(s_modx, 16)
                if isinstance(t, int) and t == FIRST:
                    load_weights(1)
                    load_weights(2)
                if has("q_y"):
                    second_halves(t, "y", "attend_y", has)
                if isinstance(t, int) and t == 0:
                    load_weights(3)
                if has("max_x1"):
                    rows(t, "x", 1)
                if has("k_x"):
                    stack(t, "x", "k", 0)
                    stack(t, "x", "q", 0)
                if has("max_y0"):
                    rows(t, "y", 0)
                if has("q_x"):
                    second_halves(t, "x", "attend_x", has)
                if has("down1"):
                    sp.wait_ge(s_y, (t - 3) * 2 + 2)
                    sp.dma_start(out[t - 3].rearrange("(a p) c -> p a c", p=128), y[:, :, :]).then_inc(s_out, 16)

            steps(sp, step)
            sp.wait_ge(s_out, 16 * B)

        @block.gpsimd
        def _(pool):
            nc.gpsimd.memset(ident[:, :], 0.0).then_inc(s_pool, 1)
            pool.wait_ge(s_pool, 1)
            nc.gpsimd.affine_select(out=ident[:, :], in_=ident[:, :], compare_op=ALU.not_equal, fill=1.0, base=0,
                                    pattern=[[-1, 128]], channel_multiplier=1).then_inc(s_ident, 1)
            nc.gpsimd.memset(V["x"][:, :, :, :], 1.0)
            nc.gpsimd.memset(V["y"][:, :, :, :], 1.0).then_inc(s_ident, 1)
            nc.gpsimd.memset(KS["x"][:, :, :].bitcast(fp32), 1.0)
            nc.gpsimd.memset(KS["y"][:, :, :].bitcast(fp32), 1.0).then_inc(s_ident, 1)
            nc.gpsimd.memset(eps[:, :], EPS)
            nc.gpsimd.memset(minus_half[:, :], -0.5).then_inc(s_ident, 1)
            pool.wait_ge(s_ident, 4)
            pool.wait_ge(s_const, 16 * 5)

            def deviation(t, stage, n):
                pool.wait_ge(s_mv, before(NORMS, t, stage) + 1)
                nc.gpsimd.tensor_tensor(var_eps[:, 0:n], mv[:, 0:n, 1], eps[:, 0:n], ALU.add).then_inc(s_eps, 1)
                pool.wait_ge(s_eps, before(NORMS, t, stage) + 1)
                nc.gpsimd.tensor_tensor(rstd[:, 0:n], var_eps[:, 0:n], minus_half[:, 0:n], ALU.pow).then_inc(s_rstd, 1)

            def hidden_low(t, u):
                pool.wait_ge(s_bank_done, before(BANK_USES, t, f"up{u}") + 1)
                nc.gpsimd.tensor_tensor(HH[:, LO, 2 * u:2 * u + 2, :], HF[:, u % 2, :, :],
                                        HH[:, HI, 2 * u:2 * u + 2, :].bitcast(fp32),
                                        ALU.subtract).then_inc(s_hidden_lo, 1)

            def step(t, has):
                if has("stats_c"):
                    deviation(t, "stats_c", 2)
                if has("up0"):
                    hidden_low(t, 0)
                    hidden_low(t, 1)
                if has("stats_y"):
                    deviation(t, "stats_y", 2)
                if has("scan_x"):
                    pool.wait_ge(s_gate_a, t * 16 + 16)
                    nc.gpsimd.tensor_tensor(gb_a[:, :], gate_a[:, :], bc_proj[:, :], ALU.mult).then_inc(s_gb_a, 1)
                    pool.wait_ge(s_x, t * 16 + 16)
                    pool.wait_ge(s_gb_a, t + 1)
                    for a in range(NB):
                        last = nc.gpsimd.tensor_tensor(x_bias[:, a, :], x_in[:, a, :], gb_a[:, :], ALU.add)
                    last.then_inc(s_x_bias, 1)
                if has("up0"):
                    hidden_low(t, 2)
                    hidden_low(t, 3)
                if has("up0"):
                    pool.wait_ge(s_gate_m, (t - 3) * 16 + 16)
                    nc.gpsimd.tensor_tensor(gb_m[:, :], gate_m[:, :], bc_mlp2[:, :], ALU.mult).then_inc(s_gb_m, 1)
                    pool.wait_ge(s_gb_m, t - 2)
                    for a in range(NB):
                        last = nc.gpsimd.tensor_tensor(x2_bias[:, a, :], x2[:, a, :], gb_m[:, :], ALU.add)
                    last.then_inc(s_x2_bias, 1)
                if has("stats_x"):
                    deviation(t, "stats_x", 2)
                if has("stats_m"):
                    deviation(t, "stats_m", 2)
                if has("stats_y"):
                    for a in range(NB):
                        last = nc.gpsimd.tensor_tensor(x1_bias[:, a, :], x1[:, a, :], bc_cproj[:, :], ALU.add)
                    last.then_inc(s_x1_bias, 1)

            steps(pool, step)

        @block.tensor
        def _(pe):
            pe.wait_ge(s_ident, 3)
            pe.wait_ge(s_small, 16 * 8)
            pe.wait_ge(s_bias_rows, 1)
            nc.tensor.transpose(scan_bank[0][:, 0:32], bias_rows, ident[0:32, 0:32])
            nc.tensor.transpose(scan_bank[0][:, 32:64], turned_rows, ident[0:32, 0:32])
            pe.wait_ge(s_silu, 1)
            for c in range(CB):
                last = nc.tensor.transpose(scan_bank[1][:, c * B:(c + 1) * B],
                                           cond_sb[:, 2, c * 128:(c + 1) * 128], ident[0:B, 0:B])
            last.then_inc(s_startT, 1)
            pe.wait_ge(s_startC, 1)
            pe.wait_ge(s_wmod, 16)
            wmod = P[:, :, :, :].rearrange("p a b c -> p (a b c)")[:, 0:CB * 6 * H].rearrange("p (c n) -> p c n", c=CB)
            for k, blk in enumerate((0, 1, 2, 3, 6, 7, 8, 9)):
                for c in range(CB):
                    last = nc.tensor.matmul(score_bank[0][:, k * B:(k + 1) * B], wmod[:, c, blk * 128:(blk + 1) * 128],
                                            silu_T[:, c, :], start=(c == 0), stop=(c == CB - 1))
            last.then_inc(s_mod, 1)
            for i in range(2):
                for c in range(CB):
                    last = nc.tensor.matmul(score_bank[1][0:B, i * H:(i + 1) * H], silu_T[:, c, :],
                                            wmod[:, c, (3 * i + 2) * H:(3 * i + 3) * H],
                                            start=(c == 0), stop=(c == CB - 1))
            last.then_inc(s_mod, 1)
            pe.wait_ge(s_modC, 2)

            def take(t, stage, use):
                wait(pe, s_bank_done, before(BANK_USES, t, stage) + use - 1)
                return bank[bank_of(t, stage, use)]

            def transposes(t, stage, use, src):
                to = take(t, stage, use)
                for c in range(CB):
                    for a in range(NB):
                        last = nc.tensor.transpose(to[:, c * N + a * 128:c * N + (a + 1) * 128],
                                                   src[:, a, c * 128:(c + 1) * 128], ident[:, :])
                last.then_inc(s_bank_full, 1)

            def columns(t, stage, use, w, xT, blocks):
                to = take(t, stage, use)
                for i, blk in enumerate(blocks):
                    n = 0
                    for c in range(CB):
                        for a, b in PARTS:
                            last = nc.tensor.matmul(to[:, i * N:(i + 1) * N], w[a][:, c, blk * 128:(blk + 1) * 128],
                                                    xT[:, b, c, :], start=(n == 0), stop=(n == 3 * CB - 1))
                            n += 1
                last.then_inc(s_bank_full, 1)

            def tokens(to, xT, w, c0, blocks, at, a):
                n = 0
                for c in range(blocks):
                    for i, j in PARTS:
                        last = nc.tensor.matmul(to[:, at:at + H], xT[:, i, c, a * 128:(a + 1) * 128],
                                                w[j][:, c, c0:c0 + H], start=(n == 0), stop=(n == 3 * blocks - 1))
                        n += 1
                return last

            def values(t, stage, w, c0, xT):
                to = take(t, stage, 0)
                for a in range(NB):
                    last = tokens(to, xT, w, c0, CB, a * H, a)
                last.then_inc(s_bank_full, 1)

            def maxima(t, stage, half):
                to = take(t, stage, 0)
                pe.wait_ge(s_max, before(MAXIMA, t, stage))
                for a in range(NB):
                    last = nc.tensor.transpose(to[0:NH, a * 128:(a + 1) * 128],
                                               MH[:, half, a, :, :, :].rearrange("p a b c -> p (a b c)").bitcast(fp32),
                                               ident[:, :])
                last.then_inc(s_bank_full, 1)

            def outputs(t, stage, w, attend):
                to = take(t, stage, 0)
                pe.wait_ge(s_OT, before(HALVES, t, f"norm_{attend}1") + 1)
                for a in range(NB):
                    last = tokens(to, OT, w, 0, 2, a * H, a)
                last.then_inc(s_bank_full, 1)

            def up(t, u):
                if u == 0:
                    pe.wait_ge(s_bank_done, before(BANK_USES, t - 1, "T_m") + 1)
                columns(t, f"up{u}", 0, w_mlp1, xT_m, (2 * u, 2 * u + 1))

            def down(t, a):
                if a == 0:
                    pe.wait_ge(s_hidden_lo, (t - 3) * 4 + 4)
                to = take(t, f"down{a}", 0)
                tokens(to, HH, w_mlp2, 0, FB, 0, a).then_inc(s_bank_full, 1)

            def transposed(t, stage, ready, count, src):
                pe.wait_ge(ready, count)
                transposes(t, stage, 0, src)

            def split_of(t, stage):
                pe.wait_ge(s_bank_done, before(BANK_USES, t, stage) + 1)

            def product(t, stage, after, w, xT, blocks):
                split_of(t, after)
                columns(t, stage, 0, w, xT, blocks)

            def weighted(t, s, grp):
                half, g = divmod(grp, 2)
                section_start = {"x3": "scan_x", "y3": "scan_y", "x": "scan_y", "y": "scan_x"}
                start = section_start[f"{s}3" if grp == 3 else s]
                pe.wait_ge(s_exp, before(ATTENDS, t, start) + (0 if grp == 3 else 4 * grp + 4))
                if g == 0:
                    later = t + 1 if (s, half) == ("x", 1) else t
                    wait(pe, s_pv_read, before(HALVES, later, f"norm_{s}{half}") - 1)
                for kb in range(NB):
                    for j in range(4):
                        last = nc.tensor.matmul(
                            pv_bank[half][32 * j:32 * j + 32, g * N:(g + 1) * N],
                            V[s][:, kb, head_of(half, g, j), :],
                            P[:, (4 * grp + j) % 8, kb, :], start=(kb == 0), stop=(kb == NB - 1))
                last.then_inc(s_pv, 1)

            tasks = {
                **{f"up{u}": lambda t, u=u: up(t, u) for u in range(FB // 2)},
                **{f"pv_{s}{g}": lambda t, s=s, g=g: weighted(t, s, g) for s in "xy" for g in range(4)},
                "v_x": lambda t: values(t, "v_x", w_qkv, 2 * H, xT_x),
                "v_y": lambda t: values(t, "v_y", w_kvc, H, xT_c),
                "out_x": lambda t: outputs(t, "out_x", w_proj, "x"),
                "T_y": lambda t: transposed(t, "T_y", s_xn_y, t, xn_a),
                "T_c": lambda t: transposed(t, "T_c", s_xn_c, t, xn_b),
                "q_y": lambda t: product(t, "q_y", "T_y", w_qc, xT_y, (0, 1)),
                "k_y": lambda t: product(t, "k_y", "T_c", w_kvc, xT_c, (0, 1)),
                "max_x0": lambda t: maxima(t, "max_x0", 0),
                "max_x1": lambda t: maxima(t, "max_x1", 1),
                "down0": lambda t: down(t, 0),
                "T_x": lambda t: transposed(t, "T_x", s_xn_x, t + 2, xn_b),
                "down1": lambda t: down(t, 1),
                "out_y": lambda t: outputs(t, "out_y", w_cproj, "y"),
                "T_m": lambda t: transposed(t, "T_m", s_xn_m, t - 1, xn_a),
                "q_x": lambda t: product(t, "q_x", "T_x", w_qkv, xT_x, (0, 1)),
                "k_x": lambda t: product(t, "k_x", "T_x", w_qkv, xT_x, (2, 3)),
                "max_y0": lambda t: maxima(t, "max_y0", 0),
                "max_y1": lambda t: maxima(t, "max_y1", 1),
            }

            def heads(letter, t, has, s1, s2):
                scan, attend = "scan_" + s1, "attend_" + s2
                scans = before(SCANS, t, scan)
                scores = before(ATTENDS, t, attend)

                def slot(s):
                    p, par = divmod(s, 2)
                    if has(scan):
                        if s % PAIRS == 0:
                            pe.wait_ge(s_load[s1][s // PAIRS], before(LOADS[s1], t, scan) * 16)
                        wait(pe, s_scan_done, scans + s - 1)
                        for a in range(NB):
                            last = nc.tensor.matmul(
                                scan_bank[s % 2][:, a * N:(a + 1) * N],
                                QS[s1][64 * par:64 * par + 3 * HD, p, a * 128:(a + 1) * 128],
                                KS[s1][64 * par:64 * par + 3 * HD, p, :], start=True, stop=True)
                        last.then_inc(s_scan_full, 1)
                    if has(attend):
                        if s % PAIRS == 0:
                            half = s // PAIRS
                            brought = before(ROWS[half], t, f"max_{s2}{half}") + 2 if half else \
                                before(ROWS[half], t, attend)
                            pe.wait_ge(s_row[half], brought * 16)
                        wait(pe, s_exp, scores + s - 1)
                        for kb in range(NB):
                            last = nc.tensor.matmul(
                                score_bank[s % 2][:, kb * N:(kb + 1) * N],
                                KS[s2][64 * par:64 * par + 3 * HD + 2, p, kb * 128:(kb + 1) * 128],
                                QS[s2][64 * par:64 * par + 3 * HD + 2, p, :], start=True, stop=True)
                        last.then_inc(s_score_full, 1)

                section(letter, t, has, slot, tasks)

            def step(t, has):
                if isinstance(t, int) and t == 1:
                    pe.wait_ge(s_weight_lo, 4)
                heads("A", t, has, "x", "y")
                if isinstance(t, int) and t == FIRST:
                    pe.wait_ge(s_weight_lo, 1)
                heads("B", t, has, "y", "x")

            steps(pe, step)

        @block.scalar
        def _(act):
            act.wait_ge(s_small, 16 * 8)
            nc.scalar.activation(cond_sb[:, 1, :], cond_sb[:, 0, :], ACT.Exp, scale=-1.0).then_inc(s_exp0, 1)

            def split_weights(i):
                act.wait_ge(s_weight[i], 16 * (2, 33, 1, 1)[i])
                for dst, src in weight_views(i, HI):
                    last = nc.scalar.activation(dst, src, ACT.Copy)
                last.then_inc(s_weight_hi, 1)

            split_weights(0)

            def full(t, stage, use=0):
                act.wait_ge(s_bank_full, before(BANK_USES, t, stage) + use + 1)
                return bank[bank_of(t, stage, use)]

            def copied(t, stage, dst):
                src = full(t, stage)
                nc.scalar.activation(dst[:, HI, :, :].rearrange("p c n -> p (c n)"), src[:, :],
                                     ACT.Copy).then_inc(s_bank_hi, 1)

            def modulated(t, stage, mod, loaded, count):
                act.wait_ge(loaded, count)
                src = full(t, stage)
                for c in range(CB):
                    last = nc.scalar.activation(xm[:, c, :], src[:, c * N:(c + 1) * N], ACT.Identity,
                                                bias=mod[:, c:c + 1], scale=mod[:, 2 + c:3 + c])
                last.then_inc(s_bank_hi, 1)

            def projected(t, stage, dst, col):
                if stage[0] == "k":
                    for s in "xy":
                        for half in range(2):
                            wait(act, s_load[s][half], before(LOADS[s], t, stage) * 16)
                src = full(t, stage)
                for i in range(2):
                    last = nc.scalar.activation(dst[:, HI, i, :], src[:, i * N:(i + 1) * N], ACT.Identity,
                                                bias=bias_cols[:, col + i:col + i + 1])
                last.then_inc(s_bank_hi, 1)

            def up(t, u):
                src = full(t, f"up{u}")
                wait(act, s_hidden_lo, (t - 3) * 4 + u - 1)
                for i in range(2):
                    col = MLPC + 2 * u + i
                    last = nc.scalar.activation(HF[:, u % 2, i, :], src[:, i * N:(i + 1) * N],
                                                ACT.Gelu_apprx_tanh, bias=bias_cols[:, col:col + 1])
                last.then_inc(s_bank_hi, 1)

            tasks = {
                **{f"up{u}": lambda t, u=u: up(t, u) for u in range(FB // 2)},
                "T_y": lambda t: copied(t, "T_y", xT_y),
                "T_c": lambda t: copied(t, "T_c", xT_c),
                "q_y": lambda t: projected(t, "q_y", SQ, 32 + QCC),
                "k_y": lambda t: projected(t, "k_y", SK, 32 + KVCC),
                "T_x": lambda t: modulated(t, "T_x", mod_x, s_modx, (t + 1) * 16 + 16),
                "T_m": lambda t: modulated(t, "T_m", mod_m, s_modm, (t - 2) * 16 + 16),
                "q_x": lambda t: projected(t, "q_x", SQ, 32 + QKVC),
                "k_x": lambda t: projected(t, "k_x", SK, 32 + QKVC + 2),
            }

            def heads(letter, t, has, attend):
                scores = before(ATTENDS, t, attend)

                def slot(s):
                    if has(attend):
                        act.wait_ge(s_score_full, scores + s + 1)
                        if s % 4 == 0:
                            group = f"pv_{attend[-1]}{s // 4 - 2}"
                            wait(act, s_pv, before(GROUPS, t, attend) if s == 0 else
                                 before(GROUPS, t, f"pv_{attend[-1]}0") if s == 4 else before(GROUPS, t, group) + 1)
                        nc.scalar.activation(P[:, s % 8, :, :].rearrange("p a n -> p (a n)"), score_bank[s % 2][:, :],
                                             ACT.Exp, scale=SCALE).then_inc(s_exp, 1)

                section(letter, t, has, slot, tasks)

            def step(t, has):
                if isinstance(t, int) and t == 0:
                    split_weights(1)
                heads("A", t, has, "attend_y")
                if isinstance(t, int) and t == 0:
                    split_weights(2)
                    split_weights(3)
                    act.wait_ge(s_weight_lo, 4)
                heads("B", t, has, "attend_x")

            steps(act, step)

        @block.vector
        def _(dve):
            nc.vector.memset(QS["x"][:, :, :].bitcast(fp32), 0.0)
            nc.vector.memset(QS["y"][:, :, :].bitcast(fp32), 0.0)
            dve.wait_ge(s_small, 16 * 8)
            nc.vector.tensor_copy(turned_rows.rearrange("p (b d h) -> p b h d", d=HD, h=PAIRS // 2),
                                  bias_rows.rearrange("p (b h d) -> p b h d", d=HD, h=PAIRS // 2))\
                .then_inc(s_bias_rows, 1)
            dve.wait_ge(s_exp0, 1)
            nc.vector.tensor_scalar_add(cond_sb[:, 2, :], cond_sb[:, 1, :], 1.0).then_inc(s_silu_part, 1)
            dve.wait_ge(s_silu_part, 1)
            nc.vector.reciprocal(cond_sb[:, 1, :], cond_sb[:, 2, :]).then_inc(s_silu_part, 1)
            dve.wait_ge(s_silu_part, 2)
            nc.vector.tensor_tensor(cond_sb[:, 2, :], cond_sb[:, 1, :], cond_sb[:, 0, :], ALU.mult).then_inc(s_silu, 1)
            dve.wait_ge(s_startT, 1)
            nc.vector.tensor_copy(bias_cols[:, :], scan_bank[0][:, 0:64])
            nc.vector.tensor_copy(silu_T[:, :, :].rearrange("p c b -> p (c b)"),
                                  scan_bank[1][:, 0:CB * B]).then_inc(s_startC, 1)
            dve.wait_ge(s_startC, 1)
            dve.wait_ge(s_mod, 1)
            for k, blk in enumerate((0, 1, 2, 3, 6, 7, 8, 9)):
                last = nc.vector.tensor_scalar(mod_all[:, :, k], score_bank[0][:, k * B:(k + 1) * B],
                                               bias_cols[:, blk:blk + 1], float(k % 4 // 2), ALU.add, ALU.add)
            last.then_inc(s_modC, 1)
            dve.wait_ge(s_mod, 2)
            dve.wait_ge(s_small, 16 * 8)
            nc.vector.tensor_tensor(gate_all, score_bank[1][0:B, :], gate_bias, ALU.add).then_inc(s_modC, 1)

            def split_weights(i):
                dve.wait_ge(s_weight_hi, i + 1)
                for (dst, src), (high, _) in zip(weight_views(i, LO), weight_views(i, HI)):
                    last = nc.vector.tensor_tensor(dst, src, high.bitcast(fp32), ALU.subtract)
                last.then_inc(s_weight_lo, 1)

            split_weights(0)
            dve.wait_ge(s_const, 16 * 5)
            dve.wait_ge(s_ident, 3)

            def link(t, stage, instruction):
                instruction.then_inc(s_link, 1)
                dve.wait_ge(s_link, before(LINKS, t, stage) + 1)

            def full(t, stage, use=0):
                dve.wait_ge(s_bank_full, before(BANK_USES, t, stage) + use + 1)
                return bank[bank_of(t, stage, use)]

            def hi_done(t, stage, use=0):
                dve.wait_ge(s_bank_hi, before(ACT_USES, t, stage) + use + 1)

            def stats_of(t, stage, inputs):
                k = 0
                for src in inputs:
                    for a in range(NB):
                        last = nc.vector.bn_stats(stats[:, k, :], src[:, a, :])
                        k += 1
                link(t, stage, last)
                nc.vector.memset(spare[:, :], 0.0)
                for i in range(k):
                    last = nc.vector.bn_aggr(mv[:, i, :], stats[:, i, :])
                last.then_inc(s_mv, 1)

            def apply(t, stage, pairs):
                dve.wait_ge(s_mv, before(NORMS, t, stage))
                dve.wait_ge(s_rstd, before(NORMS, t, stage))
                k = 0
                for src, dst, ready in pairs:
                    for a in range(NB):
                        last = nc.vector.tensor_scalar(dst[:, a, :], src[:, a, :], mv[:, k, 0:1], rstd[:, k:k + 1],
                                                       ALU.subtract, ALU.mult)
                        k += 1
                    last.then_inc(ready, 1)

            def split_modulated(t, stage, xT):
                hi_done(t, stage)
                link(t, stage, nc.vector.tensor_copy(xT[:, HI, :, :], xm[:, :, :]))
                nc.vector.tensor_tensor(xT[:, LO, :, :], xm[:, :, :], xT[:, HI, :, :].bitcast(fp32),
                                        ALU.subtract).then_inc(s_bank_done, 1)

            def split_copied(t, stage, xT):
                src = full(t, stage)
                hi_done(t, stage)
                nc.vector.tensor_tensor(xT[:, LO, :, :].rearrange("p c n -> p (c n)"), src[:, :],
                                        xT[:, HI, :, :].rearrange("p c n -> p (c n)").bitcast(fp32),
                                        ALU.subtract).then_inc(s_bank_done, 1)

            def projected(t, stage, dst, col):
                src = full(t, stage)
                hi_done(t, stage)
                for i in range(2):
                    last = nc.vector.scalar_tensor_tensor(
                        out=dst[:, LO, i, :], in0=src[:, i * N:(i + 1) * N], scalar=bias_cols[:, col + i:col + i + 1],
                        in1=dst[:, HI, i, :].bitcast(fp32), op0=ALU.add, op1=ALU.subtract)
                last.then_inc(s_bank_done, 1)

            def values(t, s):
                src = full(t, "v_" + s)
                for a in range(NB):
                    last = nc.vector.tensor_tensor(
                        V[s][:, a, :, 0:HD], src[:, a * H:(a + 1) * H].rearrange("p (h d) -> p h d", d=HD),
                        bc_v[s][:, :].rearrange("p (h d) -> p h d", d=HD), ALU.add)
                last.then_inc(s_bank_done, 1)

            def normalise(t, s, half):
                done = before(HALVES, t, f"norm_{s}{half}")

                def link_pv(n, instruction):
                    instruction.then_inc(s_link_pv, 1)
                    dve.wait_ge(s_link_pv, done * 4 + n)

                dve.wait_ge(s_pv, before(GROUPS, t, f"pv_{s}{2 * half + 1}") + 1)
                nc.vector.transpose(PT[:, :, :, :].rearrange("p a b c -> p (a b c)"), pv_bank[half][:, :])\
                    .then_inc(s_pv_read, 1)
                dve.wait_ge(s_pv_read, done + 1)
                link_pv(1, nc.vector.reciprocal(rsum[:, :, :], PT[:, :, :, HD]))
                link_pv(2, nc.vector.tensor_tensor(PN[:, :, :, :].rearrange("p b a d -> p a b d"), PT[:, :, :, 0:HD],
                                                   rsum[:, :, :].unsqueeze(3).to_broadcast([128, 2, 8, HD]), ALU.mult))
                link_pv(3, nc.vector.transpose(PO[:, :], PN[:, :, :, :].rearrange("p a b c -> p (a b c)")))
                link_pv(4, nc.vector.tensor_copy(OT[:, HI, half, :], PO[:, :]))
                nc.vector.tensor_tensor(OT[:, LO, half, :], PO[:, :], OT[:, HI, half, :].bitcast(fp32),
                                        ALU.subtract).then_inc(s_OT, 1)

            def split_maxima(t, s, half):
                step = t - 1 if (s, half) == ("y", 1) else t
                dve.wait_ge(s_scan_done, before(SCANS, step, "scan_" + s) + PAIRS * (half + 1))
                src = MX[:, :, half, :, :]
                link(t, f"split_{s}{half}", nc.vector.tensor_copy(MH[:, half, :, :, HI, :], src))
                nc.vector.tensor_tensor(MH[:, half, :, :, LO, :], src, MH[:, half, :, :, HI, :].bitcast(fp32),
                                        ALU.subtract).then_inc(s_max, 1)

            def copy_maxima(t, s, half):
                stage = f"max_{s}{half}"
                src = full(t, stage)
                wait(dve, s_row[half], before(ROWS[half], t, stage) * 16)
                nc.vector.tensor_copy(MT[half][:, :], src[0:NH, 0:N]).then_inc(s_bank_done, 1)

            def out_x(t):
                src = full(t, "out_x")
                for a in range(NB):
                    last = nc.vector.tensor_tensor(gated[:, a, :], src[:, a * H:(a + 1) * H], gate_a[:, :], ALU.mult)
                last.then_inc(s_bank_done, 1)
                dve.wait_ge(s_bank_done, before(BANK_USES, t, "out_x") + 1)
                dve.wait_ge(s_x_bias, t)
                wait(dve, s_x1_bias, t - 1)
                nc.vector.tensor_tensor(x1[:, :, :], gated[:, :, :], x_bias[:, :, :], ALU.add).then_inc(s_x1, 1)

            def out_y(t):
                src = full(t, "out_y")
                dve.wait_ge(s_x1_bias, t - 1)
                wait(dve, s_x2_bias, t - 2)
                nc.vector.tensor_tensor(x2[:, :, :].rearrange("p a c -> p (a c)"), src[:, :],
                                        x1_bias[:, :, :].rearrange("p a c -> p (a c)"),
                                        ALU.add).then_inc(s_bank_done, 1)

            def up(t, u):
                hi_done(t, f"up{u}")
                nc.vector.tensor_copy(HH[:, HI, 2 * u:2 * u + 2, :], HF[:, u % 2, :, :]).then_inc(s_bank_done, 1)

            def down(t, a):
                if a == 0:
                    dve.wait_ge(s_x2_bias, t - 2)
                    wait(dve, s_out, (t - 3) * 16)
                src = full(t, f"down{a}")
                nc.vector.tensor_tensor(y[:, a, :], src[:, 0:H], gate_m[:, :], ALU.mult).then_inc(s_bank_done, 1)
                dve.wait_ge(s_bank_done, before(BANK_USES, t, f"down{a}") + 1)
                nc.vector.tensor_tensor(y[:, a, :], y[:, a, :], x2_bias[:, a, :], ALU.add).then_inc(s_y, 1)

            def stats_c(t):
                dve.wait_ge(s_c, t * 16)
                stats_of(t, "stats_c", (c_in,))

            def stats_y(t):
                dve.wait_ge(s_x1, t)
                stats_of(t, "stats_y", (x1,))

            def stats_x(t):
                dve.wait_ge(s_x, (t + 1) * 16 + 16)
                stats_of(t, "stats_x", (x_in,))

            def stats_m(t):
                dve.wait_ge(s_bank_done, before(BANK_USES, t, "out_y") + 1)
                stats_of(t, "stats_m", (x2,))

            tasks = {
                **{f"up{u}": lambda t, u=u: up(t, u) for u in range(FB // 2)},
                **{f"norm_{s}{half}": lambda t, s=s, half=half: normalise(t, s, half)
                   for s in "xy" for half in range(2)},
                "out_x": out_x,
                "stats_y": stats_y,
                "stats_c": stats_c,
                "apply_c": lambda t: apply(t, "apply_c", ((c_in, xn_b, s_xn_c),)),
                "apply_y": lambda t: apply(t, "apply_y", ((x1, xn_a, s_xn_y),)),
                "T_y": lambda t: split_copied(t, "T_y", xT_y),
                "T_c": lambda t: split_copied(t, "T_c", xT_c),
                "q_y": lambda t: projected(t, "q_y", SQ, 32 + QCC),
                "k_y": lambda t: projected(t, "k_y", SK, 32 + KVCC),
                "split_x0": lambda t: split_maxima(t, "x", 0),
                "max_x0": lambda t: copy_maxima(t, "x", 0),
                "v_y": lambda t: values(t, "y"),
                "split_x1": lambda t: split_maxima(t, "x", 1),
                "max_x1": lambda t: copy_maxima(t, "x", 1),
                "stats_x": stats_x,
                "apply_x": lambda t: apply(t, "apply_x", ((x_in, xn_b, s_xn_x),)),
                "down0": lambda t: down(t, 0),
                "T_x": lambda t: split_modulated(t, "T_x", xT_x),
                "down1": lambda t: down(t, 1),
                "out_y": out_y,
                "stats_m": stats_m,
                "apply_m": lambda t: apply(t, "apply_m", ((x2, xn_a, s_xn_m),)),
                "T_m": lambda t: split_modulated(t, "T_m", xT_m),
                "q_x": lambda t: projected(t, "q_x", SQ, 32 + QKVC),
                "k_x": lambda t: projected(t, "k_x", SK, 32 + QKVC + 2),
                "split_y0": lambda t: split_maxima(t, "y", 0),
                "max_y0": lambda t: copy_maxima(t, "y", 0),
                "v_x": lambda t: values(t, "x"),
                "split_y1": lambda t: split_maxima(t, "y", 1),
                "max_y1": lambda t: copy_maxima(t, "y", 1),
            }

            def heads(letter, t, has, scan):
                def slot(s):
                    if has(scan):
                        p, par = divmod(s, 2)
                        half, p = divmod(p, PAIRS // 2)
                        dve.wait_ge(s_scan_full, before(SCANS, t, scan) + s + 1)
                        nc.vector.tensor_reduce(MX[:, :, half, par, p], scan_bank[s % 2][:, :].rearrange("p (a n) -> p a n", a=NB),
                                                AXIS.X, ALU.max, negate=True).then_inc(s_scan_done, 1)

                section(letter, t, has, slot, tasks, column=3)

            def step(t, has):
                if isinstance(t, int) and t == 0:
                    split_weights(1)
                heads("A", t, has, "scan_x")
                if isinstance(t, int) and t == 0:
                    split_weights(2)
                    split_weights(3)
                heads("B", t, has, "scan_y")

            steps(dve, step)


_INS = ["x", "cond_1024", "ctx_1024"] + ["L0_xcond_" + n for n in (
    "W_mod", "b_mod", "W_qkv", "b_qkv", "W_proj", "b_proj", "W_qc", "b_qc", "W_kvc", "b_kvc",
    "W_cproj", "b_cproj", "W_mlp1", "b_mlp1", "W_mlp2", "b_mlp2")]


def kernel(**inputs):
    import numpy as np
    import concourse.bacc as bacc
    from concourse.bass_utils import run_bass_kernel_spmd

    nc = bacc.Bacc("TRN2", target_bir_lowering=False, num_devices=1)
    arrays, args = {}, []
    for name in _INS:
        a = np.ascontiguousarray(inputs[name])
        arrays["in_" + name] = a
        args.append(nc.dram_tensor("in_" + name, a.shape, mybir.dt.from_np(a.dtype), kind="ExternalInput").ap())
    args.append(nc.dram_tensor("out_x", (B, N, H), fp32, kind="ExternalOutput").ap())
    build(nc, *args)
    r = run_bass_kernel_spmd(nc, [arrays], core_ids=[0])
    return r.results[0]["out_x"]
```
